# Optimizing a Trainium2 kernel written in Bass

```python
import numpy as np
import jax
import jax.numpy as jnp

def _softmax(x, axis=-1):
    return jax.nn.softmax(x, axis=axis)

def _gelu(x):
    return jax.nn.gelu(x, approximate=True)

def _silu(x):
    return jax.nn.silu(x)

def _sigmoid(x):
    return jax.nn.sigmoid(x)

def _layernorm(x, axis=-1, eps=1e-05):
    m = jnp.mean(x, axis=axis, keepdims=True)
    v = jnp.var(x, axis=axis, keepdims=True)
    return (x - m) / jnp.sqrt(v + eps)

def _scatter_add(tgt, idx, src, axis=0):
    return tgt.at[idx].add(src)

def _segment_sum(src, seg, n):
    return jax.ops.segment_sum(src, seg, n)
kernel_name = 'mk_audio_tower_d2_tok_audfeat1024_r4_d2a8c1'

def setup_inputs(seed: int=0):
    np.random.seed(seed)
    _w = jnp.asarray

    def _rec_inputs():
        import jax
        import jax.numpy as jnp
        _rk = jax.random.key(seed)
        x = -0.000125008 + 0.999885 * jax.random.normal(jax.random.fold_in(_rk, 1), (8, 750, 128), jnp.float32)
        return x
    x = _rec_inputs()

    def _L0_tok_setup():
        import jax, jax.numpy as jnp
        import numpy as np
        PT, PF = (16, 16)
        EPS = 1e-06
        key = jax.random.key(seed)
        k1, k2, k3 = jax.random.split(key, 3)
        B, T, F = (64, 1024, 128)
        E = 256
        patch_dim = PT * PF
        x = jax.random.normal(k1, (B, T, F), dtype=jnp.float32)
        W = jax.random.normal(k2, (patch_dim, E), dtype=jnp.float32) * (1.0 / np.sqrt(patch_dim))
        b = jax.random.normal(k3, (E,), dtype=jnp.float32) * 0.02
        gamma = jnp.ones((E,), dtype=jnp.float32)
        beta = jnp.zeros((E,), dtype=jnp.float32)
        return {'x': x, 'W': W, 'b': b, 'gamma': gamma, 'beta': beta}
    _L0_tok_all = _L0_tok_setup()
    _L0_tok_in = {k: v for k, v in _L0_tok_all.items() if k in ('W', 'b', 'gamma', 'beta')}
    del _L0_tok_all

    def _L0_attn_setup():
        import jax, jax.numpy as jnp
        import numpy as np
        HEADS = 16
        DIM_HEAD = 64
        B, T, C = (4, 512, 256)

        def apply_rope(x):
            d = x.shape[-1]
            seq_len = x.shape[1]
            inv_freq = 1.0 / 10000.0 ** (jnp.arange(0, d, 2, dtype=jnp.float32) / d)
            pos = jnp.arange(seq_len, dtype=jnp.float32)
            ang = pos[:, None] * inv_freq[None, :]
            sin = jnp.sin(ang)[None]
            cos = jnp.cos(ang)[None]
            x1, x2 = (x[..., 0::2], x[..., 1::2])
            rot = jnp.stack([x1 * cos - x2 * sin, x1 * sin + x2 * cos], axis=-1)
            return rot.reshape(x.shape)
        key = jax.random.key(seed)
        ks = jax.random.split(key, 6)
        inner = HEADS * DIM_HEAD
        w = 0.02
        return {'x': jax.random.normal(ks[0], (B, T, C), dtype=jnp.float32), 'Wq': jax.random.normal(ks[1], (C, inner), dtype=jnp.float32) * w, 'Wk': jax.random.normal(ks[2], (C, inner), dtype=jnp.float32) * w, 'Wv': jax.random.normal(ks[3], (C, inner), dtype=jnp.float32) * w, 'Wo': jax.random.normal(ks[4], (inner, C), dtype=jnp.float32) * w, 'bo': jnp.zeros((C,), dtype=jnp.float32)}
    _L0_attn_all = _L0_attn_setup()
    _L0_attn_in = {k: v for k, v in _L0_attn_all.items() if k in ('Wq', 'Wk', 'Wv', 'Wo', 'bo')}
    del _L0_attn_all

    def _L0_ffn_setup():
        import jax, jax.numpy as jnp
        import numpy as np
        B, S, D, F, E, K = (4, 512, 256, 1024, 4, 2)
        key = jax.random.key(seed)
        k = jax.random.split(key, 6)
        x = jax.random.normal(k[0], (B, S, D), jnp.float32)
        router_w = jax.random.normal(k[1], (D, E), jnp.float32) * D ** (-0.5)
        router_b = jnp.zeros((E,), jnp.float32)
        w1 = jax.random.normal(k[2], (E, D, F), jnp.float32) * 0.02
        w3 = jax.random.normal(k[3], (E, D, F), jnp.float32) * 0.02
        w2 = jax.random.normal(k[4], (E, F, D), jnp.float32) * 0.02
        return {'x': x, 'router_w': router_w, 'router_b': router_b, 'w1': w1, 'w3': w3, 'w2': w2}
    _L0_ffn_all = _L0_ffn_setup()
    _L0_ffn_in = {k: v for k, v in _L0_ffn_all.items() if k in ('router_w', 'router_b', 'w1', 'w3', 'w2')}
    del _L0_ffn_all

    def _L1_attn_setup():
        import jax, jax.numpy as jnp
        import numpy as np
        B, L, D = (2, 2048, 256)
        key = jax.random.key(seed)
        ks = jax.random.split(key, 6)
        x = jax.random.normal(ks[0], (B, L, D), dtype=jnp.float32)
        mag = jnp.abs(jax.random.normal(ks[1], (D,), dtype=jnp.float32))
        ang = (2.0 * np.pi * jnp.arange(D) / D).astype(jnp.float32)
        phazor_real = mag * jnp.cos(ang)
        phazor_imag = mag * jnp.sin(ang)
        phazor_init_real = jax.random.normal(ks[2], (D,), dtype=jnp.float32)
        phazor_init_imag = jax.random.normal(ks[3], (D,), dtype=jnp.float32)
        last_conv_real = jax.random.normal(ks[4], (D,), dtype=jnp.float32)
        last_conv_imag = jax.random.normal(ks[5], (D,), dtype=jnp.float32)
        return {'x': x, 'phazor_real': phazor_real, 'phazor_imag': phazor_imag, 'phazor_init_real': phazor_init_real, 'phazor_init_imag': phazor_init_imag, 'last_conv_real': last_conv_real, 'last_conv_imag': last_conv_imag}
    _L1_attn_all = _L1_attn_setup()
    _L1_attn_in = {k: v for k, v in _L1_attn_all.items() if k in ('phazor_real', 'phazor_imag', 'phazor_init_real', 'phazor_init_imag', 'last_conv_real', 'last_conv_imag')}
    del _L1_attn_all

    def _L1_ffn_setup():
        import jax, jax.numpy as jnp
        import numpy as np
        BLOCK = 32
        W_BITS = 4
        ACT_BITS = 16

        def act_qdq(x):
            qmax = 2.0 ** (ACT_BITS - 1) - 1.0
            scale = jnp.maximum(jnp.max(jnp.abs(x)) / qmax, 1e-12)
            return jnp.clip(jnp.round(x / scale), -qmax - 1.0, qmax) * scale

        def fixed_qdq_u16(x):
            scale = 1.0 / 65536.0
            return jnp.clip(jnp.round(x / scale), 0.0, 65535.0) * scale

        def lpbq_dequant(w):
            O, I = w.shape
            qmax = 2.0 ** (W_BITS - 1) - 1.0
            wb = w.reshape(O, I // BLOCK, BLOCK)
            s = jnp.maximum(jnp.max(jnp.abs(wb), axis=-1, keepdims=True) / qmax, 1e-12)
            wq = jnp.clip(jnp.round(wb / s), -qmax - 1.0, qmax) * s
            return wq.reshape(O, I)
        key = jax.random.key(seed)
        k1, k2, k3, k4 = jax.random.split(key, 4)
        B, S, H, I = (2, 1024, 256, 768)
        x = jax.random.normal(k1, (B, S, H), jnp.float32)
        w_gate = jax.random.normal(k2, (I, H), jnp.float32) * 0.02
        w_up = jax.random.normal(k3, (I, H), jnp.float32) * 0.02
        w_down = jax.random.normal(k4, (H, I), jnp.float32) * 0.02
        return {'x': x, 'w_gate': w_gate, 'w_up': w_up, 'w_down': w_down}
    _L1_ffn_all = _L1_ffn_setup()
    _L1_ffn_in = {k: v for k, v in _L1_ffn_all.items() if k in ('w_gate', 'w_up', 'w_down')}
    del _L1_ffn_all
    return {'x': x, 'L0_tok_W': _L0_tok_in['W'], 'L0_tok_b': _L0_tok_in['b'], 'L0_tok_gamma': _L0_tok_in['gamma'], 'L0_tok_beta': _L0_tok_in['beta'], 'L0_attn_Wq': _L0_attn_in['Wq'], 'L0_attn_Wk': _L0_attn_in['Wk'], 'L0_attn_Wv': _L0_attn_in['Wv'], 'L0_attn_Wo': _L0_attn_in['Wo'], 'L0_attn_bo': _L0_attn_in['bo'], 'L0_ffn_router_w': _L0_ffn_in['router_w'], 'L0_ffn_router_b': _L0_ffn_in['router_b'], 'L0_ffn_w1': _L0_ffn_in['w1'], 'L0_ffn_w3': _L0_ffn_in['w3'], 'L0_ffn_w2': _L0_ffn_in['w2'], 'L1_attn_phazor_real': _L1_attn_in['phazor_real'], 'L1_attn_phazor_imag': _L1_attn_in['phazor_imag'], 'L1_attn_phazor_init_real': _L1_attn_in['phazor_init_real'], 'L1_attn_phazor_init_imag': _L1_attn_in['phazor_init_imag'], 'L1_attn_last_conv_real': _L1_attn_in['last_conv_real'], 'L1_attn_last_conv_imag': _L1_attn_in['last_conv_imag'], 'L1_ffn_w_gate': _L1_ffn_in['w_gate'], 'L1_ffn_w_up': _L1_ffn_in['w_up'], 'L1_ffn_w_down': _L1_ffn_in['w_down']}

def reference(x, L0_tok_W, L0_tok_b, L0_tok_gamma, L0_tok_beta, L0_attn_Wq, L0_attn_Wk, L0_attn_Wv, L0_attn_Wo, L0_attn_bo, L0_ffn_router_w, L0_ffn_router_b, L0_ffn_w1, L0_ffn_w3, L0_ffn_w2, L1_attn_phazor_real, L1_attn_phazor_imag, L1_attn_phazor_init_real, L1_attn_phazor_init_imag, L1_attn_last_conv_real, L1_attn_last_conv_imag, L1_ffn_w_gate, L1_ffn_w_up, L1_ffn_w_down):
    import jax
    import jax.numpy as jnp

    def _L0_tok_ref(x, W, b, gamma, beta):
        import jax, jax.numpy as jnp
        import numpy as np
        PT, PF = (16, 16)
        EPS = 1e-06
        B, T, F = x.shape
        pad_f = -F % PF
        pad_t = -T % PT
        if pad_f or pad_t:
            x = jnp.pad(x, ((0, 0), (0, pad_t), (0, pad_f)))
            T, F = (T + pad_t, F + pad_f)
        nt, nf = (T // PT, F // PF)
        p = x.reshape(B, nt, PT, nf, PF).transpose(0, 1, 3, 2, 4).reshape(B, nt * nf, PT * PF)
        y = jnp.einsum('bpd,de->bpe', p, W) + b
        mu = jnp.mean(y, axis=-1, keepdims=True)
        var = jnp.mean(jnp.square(y - mu), axis=-1, keepdims=True)
        y = (y - mu) * jax.lax.rsqrt(var + EPS) * gamma + beta
        return y

    def _L0_attn_ref(x, Wq, Wk, Wv, Wo, bo):
        import jax, jax.numpy as jnp
        import numpy as np
        HEADS = 16
        DIM_HEAD = 64
        B, T, C = (4, 512, 256)

        def apply_rope(x):
            d = x.shape[-1]
            seq_len = x.shape[1]
            inv_freq = 1.0 / 10000.0 ** (jnp.arange(0, d, 2, dtype=jnp.float32) / d)
            pos = jnp.arange(seq_len, dtype=jnp.float32)
            ang = pos[:, None] * inv_freq[None, :]
            sin = jnp.sin(ang)[None]
            cos = jnp.cos(ang)[None]
            x1, x2 = (x[..., 0::2], x[..., 1::2])
            rot = jnp.stack([x1 * cos - x2 * sin, x1 * sin + x2 * cos], axis=-1)
            return rot.reshape(x.shape)
        b, t, c = x.shape
        h, d = (HEADS, DIM_HEAD)
        scale = d ** (-0.5)

        def split_heads(z):
            return z.reshape(b, t, h, d).transpose(0, 2, 1, 3).reshape(b * h, t, d)
        q = split_heads(x @ Wq)
        k = split_heads(x @ Wk)
        v = split_heads(x @ Wv)
        q = apply_rope(q)
        k = apply_rope(k)
        sim = jnp.einsum('bid,bjd->bij', q, k) * scale
        causal = jnp.tril(jnp.ones((t, t), dtype=bool))
        sim = jnp.where(causal[None], sim, -jnp.inf)
        attn = jax.nn.softmax(sim, axis=-1)
        out = jnp.einsum('bij,bjd->bid', attn, v)
        out = out.reshape(b, h, t, d).transpose(0, 2, 1, 3).reshape(b, t, h * d)
        return out @ Wo + bo

    def _L0_ffn_ref(x, router_w, router_b, w1, w3, w2):
        import jax, jax.numpy as jnp
        import numpy as np
        B, S, D, F, E, K = (4, 512, 256, 1024, 4, 2)
        b, s, d = x.shape
        T = b * s
        e = router_w.shape[1]
        xf = x.reshape(T, d)
        logits = xf @ router_w + router_b
        probs = jax.nn.softmax(logits, axis=-1)
        top_p, top_i = jax.lax.top_k(probs, K)
        top_p = top_p / jnp.sum(top_p, axis=-1, keepdims=True)
        gates = jnp.zeros((T, e), xf.dtype).at[jnp.arange(T)[:, None], top_i].add(top_p)
        h = jax.nn.silu(jnp.einsum('td,edf->etf', xf, w1)) * jnp.einsum('td,edf->etf', xf, w3)
        expert_out = jnp.einsum('etf,efd->etd', h, w2)
        out = jnp.einsum('te,etd->td', gates, expert_out)
        return out.reshape(b, s, d)

    def _L1_attn_ref(x, phazor_real, phazor_imag, phazor_init_real, phazor_init_imag, last_conv_real, last_conv_imag):
        import jax, jax.numpy as jnp
        import numpy as np
        B, L, D = (2, 2048, 256)
        b, length, dim = x.shape
        dtype = x.dtype
        ph = jnp.exp(-(phazor_real * phazor_real + phazor_imag * phazor_imag)) * jnp.exp(1j * jnp.arctan2(phazor_imag, phazor_real))
        prog = jnp.power(ph[None, :], jnp.arange(length)[:, None])
        pinit = phazor_init_real + 1j * phazor_init_imag
        filt = prog * pinit[None, :]
        filt_fft = jnp.fft.fft(filt, n=2 * length, axis=0)
        x_fft = jnp.fft.fft(x.astype(jnp.complex64), n=2 * length, axis=1)
        conv = jnp.fft.ifft(filt_fft[None, :, :] * x_fft, axis=1)[:, :length, :]
        last = (last_conv_real + 1j * last_conv_imag)[None, None, :]
        conv_with_past = conv + last * prog[None, :, :] * ph[None, None, :]
        return conv_with_past.real.astype(dtype)

    def _L1_ffn_ref(x, w_gate, w_up, w_down):
        import jax, jax.numpy as jnp
        import numpy as np
        BLOCK = 32
        W_BITS = 4
        ACT_BITS = 16

        def act_qdq(x):
            qmax = 2.0 ** (ACT_BITS - 1) - 1.0
            scale = jnp.maximum(jnp.max(jnp.abs(x)) / qmax, 1e-12)
            return jnp.clip(jnp.round(x / scale), -qmax - 1.0, qmax) * scale

        def fixed_qdq_u16(x):
            scale = 1.0 / 65536.0
            return jnp.clip(jnp.round(x / scale), 0.0, 65535.0) * scale

        def lpbq_dequant(w):
            O, I = w.shape
            qmax = 2.0 ** (W_BITS - 1) - 1.0
            wb = w.reshape(O, I // BLOCK, BLOCK)
            s = jnp.maximum(jnp.max(jnp.abs(wb), axis=-1, keepdims=True) / qmax, 1e-12)
            wq = jnp.clip(jnp.round(wb / s), -qmax - 1.0, qmax) * s
            return wq.reshape(O, I)
        x = act_qdq(x)
        up = act_qdq(x @ lpbq_dequant(w_up).T)
        gate = act_qdq(x @ lpbq_dequant(w_gate).T)
        sig = fixed_qdq_u16(jax.nn.sigmoid(gate))
        gate = act_qdq(gate * sig)
        o = act_qdq(gate * up)
        return o @ lpbq_dequant(w_down).T
    h = _L0_tok_ref(x, L0_tok_W, L0_tok_b, L0_tok_gamma, L0_tok_beta)
    h = h + _L0_attn_ref(_layernorm(h, axis=-1), L0_attn_Wq, L0_attn_Wk, L0_attn_Wv, L0_attn_Wo, L0_attn_bo)
    h = h + _L0_ffn_ref(_layernorm(h, axis=-1), L0_ffn_router_w, L0_ffn_router_b, L0_ffn_w1, L0_ffn_w3, L0_ffn_w2)
    h = h + _L1_attn_ref(_layernorm(h, axis=-1), L1_attn_phazor_real, L1_attn_phazor_imag, L1_attn_phazor_init_real, L1_attn_phazor_init_imag, L1_attn_last_conv_real, L1_attn_last_conv_imag)
    h = h + _L1_ffn_ref(_layernorm(h, axis=-1), L1_ffn_w_gate, L1_ffn_w_up, L1_ffn_w_down)
    return h

_drawn_inputs = setup_inputs


def setup_inputs(seed=0):
    import zlib

    import numpy as np

    out = dict(_drawn_inputs(seed))
    spreads = {'L0_tok_gamma': (1.0, 0.2),
     'L0_tok_beta': (0.0, 0.1),
     'L0_attn_bo': (0.0, 0.1),
     'L0_ffn_router_b': (0.0, 0.8)}
    factors = {'L0_tok_b': 3.627,
     'L0_attn_Wq': 8.0,
     'L0_attn_Wk': 8.0,
     'L0_ffn_router_w': 2.756,
     'L1_ffn_w_gate': 6.161,
     'L1_ffn_w_up': 6.038,
     'L1_ffn_w_down': 6.089}
    for name, (base, spread) in spreads.items():
        noise = np.random.default_rng([zlib.crc32(name.encode()), seed]).standard_normal(out[name].shape)
        drawn = base * np.exp(spread * noise) if base else spread * noise
        out[name] = jnp.asarray(drawn.astype(out[name].dtype))
    for name, factor in factors.items():
        out[name] = (out[name] * factor).astype(out[name].dtype)
    return out
```

```python
from contextlib import ExitStack

import numpy as np

import concourse.bass as bass
from concourse import mybir
from concourse.alu_op_type import AluOpType as ALU

F32 = mybir.dt.float32
F32R = mybir.dt.float32r
BF16 = mybir.dt.bfloat16
ACT = mybir.ActivationFunctionType
AX_X = mybir.AxisListType.X
AX_XY = mybir.AxisListType.XY

P = 128
BATCH = 8
TIME, FREQ = 750, 128
PATCH = 16
TOK = -(-TIME // PATCH) * (FREQ // PATCH)
TOKENS = BATCH * TOK
DIM = 256
HALVES = DIM // P
HEADS, HEAD = 16, 64
INNER = HEADS * HEAD
PAIRS = HEADS // 2
EXPERTS, FFN = 4, 1024
QFFN, QBLOCK = 768, 32
TILES = -(-TOK // P)
TILE_ROWS = [min(P, TOK - P * i) for i in range(TILES)]
BANK = 512
NEG = -1e30

VECTORS = ("L0_tok_b", "L0_tok_gamma", "L0_tok_beta", "L0_attn_bo", "L1_attn_phazor_real",
           "L1_attn_phazor_imag", "L1_attn_phazor_init_real", "L1_attn_phazor_init_imag",
           "L1_attn_last_conv_real", "L1_attn_last_conv_imag")
EPS_TOK, EPS_LN, PLUS_MAGIC, MINUS_MAGIC = range(4)


def scopes(nc):
    ctx = ExitStack()
    sb = lambda name, shape, dt=F32: ctx.enter_context(nc.sbuf_tensor(name, shape, dt))
    sem = lambda name: ctx.enter_context(nc.semaphore(name))
    return ctx, sb, sem


def clear(nc, sems):
    with nc.Block() as block:
        @block.gpsimd
        def _(pool):
            for s in sems:
                pool.sem_clear(s)


def tokens_of(n):
    return bass.ds(n * TOK, TOK)


def tokenize(nc, psum, hid, patches_dram, w_dram, bias):
    ctx, sb, sem = scopes(nc)
    with ctx:
        patch = sb("patch", [P, 2, TOKENS])
        w = sb("tok_w", [P, 2, DIM])
        loaded = [sem(f"tok_loaded{i}") for i in range(2)]
        params, made, kept = sem("tok_params"), sem("tok_made"), sem("tok_kept")
        with nc.Block() as block:
            @block.sync
            def _(sp):
                sp.dma_start(w[:], w_dram.rearrange("(c p) e -> p c e", p=P)).then_inc(params, 16)
                half = TOKENS // 2
                for i in range(2):
                    sp.dma_start(patch[:, :, i * half:(i + 1) * half],
                                 patches_dram[:, :, i * half:(i + 1) * half]).then_inc(loaded[i], 16)

            @block.tensor
            def _(pe):
                pe.wait_ge(params, 16)
                for part in range(2):
                    pe.wait_ge(loaded[part], 16)
                    with pe.Fori(part * 2, part * 2 + 2) as i:
                        for u in range(2):
                            pe.wait_ge(kept, 2 * i + u + 1)
                            for m in range(HALVES):
                                for c in range(2):
                                    last = pe.matmul(psum[:, 2 * u + m, 0:TOK], w[:, c, m * P:(m + 1) * P],
                                                     patch[:, c, tokens_of(2 * i + u)],
                                                     start=(c == 0), stop=(c == 1))
                            last.then_inc(made, 1)

            @block.scalar
            def _(act):
                act.sem_inc(kept, 2)
                with act.Fori(0, BATCH // 2) as i:
                    for u in range(2):
                        act.wait_ge(made, 2 * i + u + 1)
                        for m in range(HALVES):
                            last = act.activation(hid[:, m, tokens_of(2 * i + u)], psum[:, 2 * u + m, 0:TOK],
                                                  ACT.Identity, bias=bias[:, m:m + 1])
                        last.then_inc(kept, 1)


def layernorm(nc, psum, sems, name, src, dst, consts, ones, eps, affine=None):
    ctx, sb, sem = scopes(nc)
    with ctx:
        square = sb(f"{name}_square", [P, 2, HALVES, TOK])
        std = sb(f"{name}_std", [P, 2, TOK])
        rstd = sb(f"{name}_rstd", [P, 2, TOK])
        mean_made, centered, squared, var_made, std_made, rstd_made, normed = sems
        clear(nc, sems)
        with nc.Block() as block:
            @block.tensor
            def _(pe):
                pe.sem_inc(var_made, 2)
                with pe.Fori(0, BATCH // 2) as i:
                    for u in range(2):
                        pe.wait_ge(centered, 2 * i + u + 1)
                        for c in range(HALVES):
                            last = pe.matmul(psum[:, u, 0:TOK], ones[:], src[:, c, tokens_of(2 * i + u)],
                                             start=(c == 0), stop=(c == HALVES - 1))
                        last.then_inc(mean_made, 1)
                    for u in range(2):
                        pe.wait_ge(std_made, 2 * i + u + 1)
                        pe.wait_ge(squared, 2 * i + u + 1)
                        for c in range(HALVES):
                            last = pe.matmul(psum[:, 2 + u, 0:TOK], ones[:], square[:, u, c, :],
                                             start=(c == 0), stop=(c == HALVES - 1))
                        last.then_inc(var_made, 1)

            @block.vector
            def _(dve):
                dve.sem_inc(centered, 2)
                dve.sem_inc(rstd_made, 2)
                with dve.Fori(0, BATCH // 2) as i:
                    for u in range(2):
                        dve.wait_ge(mean_made, 2 * i + u + 1)
                        t = tokens_of(2 * i + u)
                        dve.tensor_tensor(dst[:, :, t], src[:, :, t],
                                          psum[:, u:u + 1, 0:TOK].broadcast_to((P, HALVES, TOK)),
                                          ALU.subtract).then_inc(centered, 1)
                    for u in range(2):
                        dve.wait_ge(std_made, 2 * i + u + 3)
                        dve.reciprocal(rstd[:, u, :], std[:, u, :]).then_inc(rstd_made, 1)
                        dve.wait_ge(rstd_made, 2 * i + u + 3)
                        t = tokens_of(2 * i + u)
                        dve.tensor_tensor(dst[:, :, t], dst[:, :, t],
                                          rstd[:, u:u + 1, :].broadcast_to((P, HALVES, TOK)),
                                          ALU.mult).then_inc(normed, 1)

            @block.scalar
            def _(act):
                act.sem_inc(std_made, 2)
                with act.Fori(0, BATCH // 2) as i:
                    for u in range(2):
                        act.wait_ge(centered, 2 * i + u + 3)
                        act.wait_ge(var_made, 2 * i + u + 1)
                        act.activation(square[:, u, :, :], dst[:, :, tokens_of(2 * i + u)],
                                       ACT.Square).then_inc(squared, 1)
                    for u in range(2):
                        act.wait_ge(var_made, 2 * i + u + 3)
                        act.wait_ge(rstd_made, 2 * i + u + 1)
                        act.activation(std[:, u, :], psum[:, 2 + u, 0:TOK], ACT.Sqrt,
                                       bias=consts[:, eps:eps + 1]).then_inc(std_made, 1)
                if affine is not None:
                    gamma, beta = affine
                    with act.Fori(0, BATCH) as n:
                        act.wait_ge(normed, n + 1)
                        for c in range(HALVES):
                            act.activation(dst[:, c, tokens_of(n)], dst[:, c, tokens_of(n)], ACT.Identity,
                                           scale=gamma[:, c:c + 1], bias=beta[:, c:c + 1])


def split_weights(nc, name, jobs, waits=()):
    ctx, sb, sem = scopes(nc)
    with ctx:
        stage = [sb(f"{name}_stage{i}", [P, *jobs[i][0].shape[1:]]) for i in range(len(jobs))]
        arrived = [sem(f"{name}_arrived{i}") for i in range(len(jobs))]
        high_made, low_made = sem(f"{name}_high"), sem(f"{name}_low")
        with nc.Block() as block:
            @block.sync
            def _(sp):
                for i, (src, _, _) in enumerate(jobs):
                    sp.dma_start(stage[i][:], src).then_inc(arrived[i], 16)

            @block.scalar
            def _(act):
                for i, (_, high, _) in enumerate(jobs):
                    act.wait_ge(arrived[i], 16)
                    act.activation(high, stage[i][:], ACT.Copy).then_inc(high_made, 1)

            @block.vector
            def _(dve):
                for i, (_, high, low) in enumerate(jobs):
                    dve.wait_ge(high_made, i + 1)
                    dve.tensor_tensor(low, stage[i][:], high.bitcast(F32), ALU.subtract).then_inc(low_made, 1)


def attention(nc, psum, norm, hid_dram, a, consts, ident, bo):
    ctx, sb, sem = scopes(nc)
    with ctx:
        wq, wk, wv = ([sb(f"{n}_{part}", [P, 2, INNER], F32R) for part in ("high", "low")]
                      for n in ("wq", "wk", "wv"))
        wo = [sb(f"wo_{part}", [P, PAIRS, DIM], F32R) for part in ("high", "low")]
        rows = lambda d: d.rearrange("(c p) n -> p c n", p=P)
        split_weights(nc, "attn_w", [(rows(a["L0_attn_Wq"]), wq[0][:], wq[1][:]),
                                     (rows(a["L0_attn_Wk"]), wk[0][:], wk[1][:]),
                                     (rows(a["L0_attn_Wv"]), wv[0][:], wv[1][:]),
                                     (rows(a["L0_attn_Wo"]), wo[0][:], wo[1][:])])

        x = [sb(f"x_{part}", [P, 2, TOK], F32R) for part in ("high", "low")]
        v = [sb(f"v_{part}", [P, TILES, INNER], F32R) for part in ("high", "low")]
        qk = [sb(f"qk_{part}", [P, 2, 2, TOK], F32R) for part in ("high", "low")]
        raw = sb("raw", [P, 2, TOK])
        swapped = sb("swapped", [P, 2, TOK])
        cosined = sb("cosined", [P, 2, TOK])
        rotated = sb("rotated", [P, 2, TOK])
        cos = sb("rope_cos", [P, 2, TOK])
        sin = sb("rope_sin", [P, 2, TOK])
        neg_max = sb("neg_max", [P, 2, 4])
        row_sum = sb("row_sum", [P, 2, 4])
        inv_sum = sb("inv_sum", [P, 2, 4])
        probs = sb("probs", [P, 2, TILES, TOK])
        diag = sb("diag", [P, 2, TILES, P])
        pt = [sb(f"pt_{part}", [P, 2, 2, TOK], F32R) for part in ("high", "low")]
        o = [sb(f"o_{part}", [P, PAIRS, TOK], F32R) for part in ("high", "low")]
        resid = sb("resid", [P, HALVES, TOK])
        mask = sb("mask", [P, P], BF16)
        ident_b = sb("ident_b", [P, P], BF16)
        mask_f = sb("mask_f", [P, P])
        holder = sb("holder", [P, 2 * PAIRS])
        (tables_in, masks_made, resid_in, cleared, x_high, x_low, v_made, v_high, v_low, proj_made,
         raw_made, swap_made, rope_made, rot_made, qk_high, qk_ready, scores_made, max_made, exp_made,
         inv_made, diag_made, turned, pt_high, pt_ready, mixed, o_high, o_ready, out_made, out_kept) = (
            sem(n) for n in
            "tables_in masks_made resid_in cleared x_high x_low v_made v_high v_low proj_made "
            "raw_made swap_made rope_made rot_made qk_high qk_ready scores_made max_made exp_made "
            "inv_made diag_made turned pt_high pt_ready mixed o_high o_ready out_made out_kept".split())
        CR_RAW, CR_ROT, CR_SCORES, CR_EXP, CR_TURN, CR_PT, CR_MIX, CR_O, CR_OUT = 1, 2, 4, 2, 2, 1, 2, 1, 1
        BANK_PROJ, BANK_O, BANK_PT, OUT_BANKS = 7, 6, 4, (6, 2)
        three = ((0, 0), (0, 1), (1, 0))
        swap = [i ^ 1 for i in range(32)]

        def score_bank(par, it):
            if it == 2:
                return psum[0:TILE_ROWS[2], 2 * par + 1, 0:TOK]
            return psum[:, 2 * par, P * it:P * it + P * (it + 1)]

        def probs_t(j):
            return (0, 0, TOK) if j == 0 else (1, 0, TOK - P) if j == 1 else (1, TOK - P, TOK - 2 * P)

        with nc.Block() as block:
            @block.sync
            def _(sp):
                sp.dma_start(cos[:], a["c_cos"]).then_inc(tables_in, 16)
                sp.dma_start(sin[:], a["c_sin"]).then_inc(tables_in, 16)
                sp.dma_start(mask_f[:], a["c_mask"]).then_inc(tables_in, 16)
                with sp.Fori(0, BATCH) as b:
                    sp.wait_ge(out_kept, 2 * b + CR_OUT)
                    sp.dma_start(resid[:], hid_dram[:, :, tokens_of(b)]).then_inc(resid_in, 16)

            AHEAD = 6

            @block.tensor
            def _(pe):
                pe.sem_inc(scores_made, CR_SCORES)
                pe.sem_inc(turned, CR_TURN)
                pe.sem_inc(mixed, CR_MIX)
                pe.wait_ge(masks_made, 2)
                pe.wait_ge(cleared, 3)

                def project(b, n):
                    c, k = n // 2, n % 2
                    pe.wait_ge(raw_made, 16 * b + n + CR_RAW)
                    w = (wq, wk)[k]
                    for i, (hw, hx) in enumerate(three):
                        for half in range(2):
                            last = pe.matmul(psum[:, BANK_PROJ, 0:TOK], w[hw][:, half, P * c:P * (c + 1)],
                                             x[hx][:, half, :], start=(i == half == 0), stop=(i == 2 and half == 1))
                    last.then_inc(proj_made, 1)

                def scores(b, h):
                    c, par = h // 2, h % 2
                    r = slice(HEAD * par, HEAD * (par + 1))
                    pe.wait_ge(qk_ready, 16 * b + 2 * c + 2)
                    pe.wait_ge(exp_made, 16 * b + h + 1)
                    for it in range(TILES):
                        ni, dst = TILE_ROWS[it], score_bank(par, it)
                        nj = P * it + ni
                        for i, (hq, hk) in enumerate(three):
                            pe.matmul(dst, qk[hq][r, c % 2, 0, P * it:P * it + ni], qk[hk][r, c % 2, 1, 0:nj],
                                      start=(i == 0), stop=False)
                        last = pe.matmul(dst[:, P * it:nj], ident_b[:, 0:ni], mask[:, 0:ni],
                                         start=False, stop=True)
                    last.then_inc(scores_made, 1)

                def turn(b, h):
                    pe.wait_ge(diag_made, 16 * b + h + 1)
                    pe.wait_ge(pt_ready, 16 * b + h + CR_PT)
                    for j in range(TILES):
                        bank, col, _ = probs_t(j)
                        for it in range(j, TILES):
                            ni, nj = TILE_ROWS[it], TILE_ROWS[j]
                            at = col + P * (it - j)
                            last = pe.matmul(psum[0:nj, BANK_PT + bank, at:at + ni],
                                             probs[0:ni, h % 2, it, P * j:P * j + nj],
                                             diag[0:ni, h % 2, it, 0:ni], start=True, stop=True)
                    last.then_inc(turned, 1)

                def mix(b, h):
                    c = h // 2
                    pe.wait_ge(pt_ready, 16 * b + h + 1 + CR_PT)
                    pe.wait_ge(o_ready, 16 * b + h + CR_O)
                    for j in range(TILES):
                        bank, col, n = probs_t(j)
                        for i, (hv, hp) in enumerate(three):
                            nj = TILE_ROWS[j]
                            last = pe.matmul(psum[:, BANK_O, P * j:TOK], v[hv][0:nj, j, P * c:P * (c + 1)],
                                             pt[hp][0:nj, h % 2, bank, col:col + n],
                                             start=(i == j == 0), stop=(i == 2 and j == TILES - 1))
                    last.then_inc(mixed, 1)

                def values(b):
                    pe.wait_ge(x_low, b + 1)
                    pe.wait_ge(exp_made, 16 * b + CR_EXP)
                    pe.wait_ge(pt_ready, 16 * b + CR_PT)
                    for t in range(TILES):
                        for half in range(2):
                            for i, (hw, hx) in enumerate(three):
                                for c in range(2):
                                    last = pe.matmul(psum[0:TILE_ROWS[t], 2 * t + half, :],
                                                     x[hx][:, c, P * t:P * t + TILE_ROWS[t]],
                                                     wv[hw][:, c, BANK * half:BANK * (half + 1)],
                                                     start=(i == c == 0), stop=(i == 2 and c == 1))
                            last.then_inc(v_made, 1)

                def output(b, m):
                    if m == 0:
                        pe.wait_ge(o_ready, 16 * b + HEADS + CR_O)
                    else:
                        pe.wait_ge(v_low, 6 * b + 12)
                    for i, (hw, ho) in enumerate(three):
                        for c in range(PAIRS):
                            last = pe.matmul(psum[:, OUT_BANKS[m], 0:TOK], wo[hw][:, c, P * m:P * (m + 1)],
                                             o[ho][:, c, :], start=(i == c == 0), stop=(i == 2 and c == PAIRS - 1))
                    last.then_inc(out_made, 1)

                def begin(b, before=None):
                    values(b)
                    project(b, 0)
                    if before is not None:
                        output(before, 0)
                    project(b, 1)
                    if before is not None:
                        output(before, 1)
                    project(b, 2)
                    pe.wait_ge(v_low, 6 * b + 6)
                    project(b, 3)
                    scores(b, 0)
                    project(b, 4)
                    if before is not None:
                        pe.wait_ge(out_kept, 2 * b + CR_OUT)
                    scores(b, 1)
                    project(b, 5)

                def heads(b):
                    for h in range(HEADS):
                        turn(b, h)
                        if h + 2 < HEADS:
                            scores(b, h + 2)
                        if h:
                            mix(b, h - 1)
                        if h + AHEAD < HEADS:
                            project(b, h + AHEAD)
                    mix(b, HEADS - 1)

                begin(0)
                with pe.Fori(0, BATCH - 1) as b:
                    heads(b)
                    begin(b + 1, b)
                heads(BATCH - 1)
                output(BATCH - 1, 0)
                for i, (hw, ho) in enumerate(three):
                    for c in range(PAIRS):
                        last = pe.matmul(psum[:, OUT_BANKS[1], 0:TOK], wo[hw][:, c, P:2 * P],
                                         o[ho][:, c, :], start=(i == c == 0), stop=(i == 2 and c == PAIRS - 1))
                last.then_inc(out_made, 1)

            @block.scalar
            def _(act):
                act.sem_inc(exp_made, CR_EXP)
                act.sem_inc(raw_made, CR_RAW)

                def x_split(b):
                    act.activation(x[0][:], norm[:, :, tokens_of(b)], ACT.Copy).then_inc(x_high, 1)

                def raw_copy(b, n):
                    act.wait_ge(proj_made, 16 * b + n + 1)
                    act.wait_ge(rot_made, 16 * b + n + 1)
                    act.activation(raw[:, n % 2, :], psum[:, BANK_PROJ, 0:TOK], ACT.Copy).then_inc(raw_made, 1)

                def qk_split(b, n):
                    c = n // 2
                    act.wait_ge(rot_made, 16 * b + n + 1 + CR_ROT)
                    act.wait_ge(scores_made, 16 * b + 2 * c + CR_SCORES - 2)
                    act.activation(qk[0][:, c % 2, n % 2, :], rotated[:, n % 2, :], ACT.Copy).then_inc(qk_high, 1)

                def exps(b, h):
                    act.wait_ge(max_made, 16 * b + h + 1)
                    act.wait_ge(turned, 16 * b + h + 1)
                    for it in range(TILES):
                        ni = TILE_ROWS[it]
                        last = act.activation(probs[0:ni, h % 2, it, 0:P * it + ni], score_bank(h % 2, it),
                                              ACT.Exp, bias=neg_max[0:ni, h % 2, it:it + 1],
                                              accum_out=row_sum[0:ni, h % 2, it:it + 1])
                    last.then_inc(exp_made, 1)

                def turned_high(b, h):
                    act.wait_ge(turned, 16 * b + h + 1 + CR_TURN)
                    act.wait_ge(mixed, 16 * b + h + 1)
                    act.activation(pt[0][:, h % 2, :, :], psum[:, BANK_PT:BANK_PT + 2, 0:TOK],
                                   ACT.Copy).then_inc(pt_high, 1)

                def out_high(b, h):
                    r = slice(HEAD * (h % 2), HEAD * (h % 2 + 1))
                    act.wait_ge(mixed, 16 * b + h + 1 + CR_MIX)
                    act.activation(o[0][r, h // 2, :], psum[r, BANK_O, 0:TOK], ACT.Copy).then_inc(o_high, 1)

                def begin(b):
                    for t in range(TILES):
                        for half in range(2):
                            act.wait_ge(v_made, 6 * b + 2 * t + half + 1)
                            act.activation(v[0][0:TILE_ROWS[t], t, BANK * half:BANK * (half + 1)],
                                           psum[0:TILE_ROWS[t], 2 * t + half, :], ACT.Copy).then_inc(v_high, 1)
                    raw_copy(b, 0)
                    raw_copy(b, 1)
                    qk_split(b, 0)
                    raw_copy(b, 2)
                    qk_split(b, 1)
                    raw_copy(b, 3)
                    qk_split(b, 2)
                    raw_copy(b, 4)
                    qk_split(b, 3)
                    exps(b, 0)
                    raw_copy(b, 5)

                def heads(b, more):
                    for h in range(HEADS):
                        if h + 1 < HEADS:
                            exps(b, h + 1)
                        turned_high(b, h)
                        if h:
                            out_high(b, h - 1)
                        if h + AHEAD - 2 < HEADS:
                            qk_split(b, h + AHEAD - 2)
                        if h + AHEAD < HEADS:
                            raw_copy(b, h + AHEAD)
                        if h == HEADS - 4 and more:
                            act.wait_ge(proj_made, 16 * b + 2 * PAIRS)
                            x_split(b + 1)
                    out_high(b, HEADS - 1)

                act.wait_ge(cleared, 3)
                x_split(0)
                begin(0)
                with act.Fori(0, BATCH - 1) as b:
                    heads(b, True)
                    begin(b + 1)
                heads(BATCH - 1, False)

            @block.gpsimd
            def _(pool):
                pool.sem_inc(rot_made, CR_ROT)

                def qk_split(b, n):
                    c, k = n // 2, n % 2
                    pool.wait_ge(qk_high, 16 * b + n + 1)
                    pool.tensor_tensor(qk[1][:, c % 2, k, :], rotated[:, k, :],
                                       qk[0][:, c % 2, k, :].bitcast(F32), ALU.subtract).then_inc(qk_ready, 1)

                pool.wait_ge(tables_in, 48)
                with pool.Fori(0, BATCH) as b:
                    for n in range(2 * PAIRS):
                        k = n % 2
                        pool.wait_ge(raw_made, 16 * b + n + 1 + CR_RAW)
                        pool.tensor_tensor(cosined[:, k, :], raw[:, k, :], cos[:, k, :],
                                           ALU.mult).then_inc(rope_made, 1)
                        pool.wait_ge(swap_made, 16 * b + n + 1)
                        pool.tensor_tensor(swapped[:, k, :], swapped[:, k, :], sin[:, k, :],
                                           ALU.mult).then_inc(rope_made, 1)
                        pool.wait_ge(rope_made, 32 * b + 2 * n + 2)
                        pool.tensor_tensor(rotated[:, k, :], cosined[:, k, :], swapped[:, k, :],
                                           ALU.add).then_inc(rot_made, 1)
                        if n:
                            qk_split(b, n - 1)
                    qk_split(b, 2 * PAIRS - 1)

            @block.vector
            def _(dve):
                dve.sem_inc(pt_ready, CR_PT)
                dve.sem_inc(o_ready, CR_O)
                dve.sem_inc(out_kept, CR_OUT)
                dve.memset(row_sum[:], 1.0).then_inc(cleared, 1)
                dve.memset(psum[:, BANK_PT:BANK_PT + 2, 0:TOK], 0.0).then_inc(cleared, 1)
                dve.memset(neg_max[:], 0.0).then_inc(cleared, 1)
                dve.wait_ge(tables_in, 48)
                dve.tensor_copy(mask[:], mask_f[:]).then_inc(masks_made, 1)
                dve.tensor_copy(ident_b[:], ident[:]).then_inc(masks_made, 1)
                dve.wait_ge(cleared, 3)

                def x_split(b):
                    dve.wait_ge(x_high, b + 1)
                    dve.tensor_tensor(x[1][:], norm[:, :, tokens_of(b)], x[0][:].bitcast(F32),
                                      ALU.subtract).then_inc(x_low, 1)

                def swap_pairs(b, n):
                    dve.wait_ge(raw_made, 16 * b + n + 1 + CR_RAW)
                    dve.memset(holder[:, n:n + 1], 0.0)
                    dve.stream_shuffle(swapped[:, n % 2, :], raw[:, n % 2, :], swap).then_inc(swap_made, 1)

                def maxima(b, h):
                    dve.wait_ge(scores_made, 16 * b + h + 1 + CR_SCORES)
                    for it in range(TILES):
                        ni = TILE_ROWS[it]
                        last = dve.tensor_reduce(neg_max[0:ni, h % 2, it:it + 1], score_bank(h % 2, it),
                                                 AX_X, ALU.max, negate=True)
                    last.then_inc(max_made, 1)

                def diagonals(b, h):
                    dve.wait_ge(exp_made, 16 * b + h + 1 + CR_EXP)
                    dve.reciprocal(inv_sum[:, h % 2, 0:TILES], row_sum[:, h % 2, 0:TILES]).then_inc(inv_made, 1)
                    dve.wait_ge(inv_made, 16 * b + h + 1)
                    dve.tensor_tensor(diag[:, h % 2, :, :],
                                      ident[:].rearrange("p (o n) -> p o n", o=1).broadcast_to((P, TILES, P)),
                                      inv_sum[:, h % 2, 0:TILES].rearrange("p (t o) -> p t o", o=1)
                                      .broadcast_to((P, TILES, P)), ALU.mult).then_inc(diag_made, 1)

                def turned_low(b, h):
                    dve.wait_ge(pt_high, 16 * b + h + 1)
                    dve.tensor_tensor(pt[1][:, h % 2, :, :], psum[:, BANK_PT:BANK_PT + 2, 0:TOK],
                                      pt[0][:, h % 2, :, :].bitcast(F32), ALU.subtract).then_inc(pt_ready, 1)

                def out_low(b, h):
                    r = slice(HEAD * (h % 2), HEAD * (h % 2 + 1))
                    dve.wait_ge(o_high, 16 * b + h + 1)
                    dve.tensor_tensor(o[1][r, h // 2, :], psum[r, BANK_O, 0:TOK],
                                      o[0][r, h // 2, :].bitcast(F32), ALU.subtract).then_inc(o_ready, 1)

                def residual(b, m):
                    dve.wait_ge(out_made, 2 * b + m + 1)
                    dve.wait_ge(resid_in, 16 * b + 16)
                    dve.scalar_tensor_tensor(norm[:, m, tokens_of(b)], psum[:, OUT_BANKS[m], 0:TOK],
                                             bo[:, m:m + 1], resid[:, m, :], ALU.add, ALU.add).then_inc(out_kept, 1)

                def begin(b, before=None):
                    for t in range(TILES):
                        for half in range(2):
                            dve.wait_ge(v_high, 6 * b + 2 * t + half + 1)
                            cols = slice(BANK * half, BANK * (half + 1))
                            dve.tensor_tensor(v[1][0:TILE_ROWS[t], t, cols],
                                              psum[0:TILE_ROWS[t], 2 * t + half, :],
                                              v[0][0:TILE_ROWS[t], t, cols].bitcast(F32),
                                              ALU.subtract).then_inc(v_low, 1)
                    swap_pairs(b, 0)
                    if before is not None:
                        residual(before, 0)
                    swap_pairs(b, 1)
                    swap_pairs(b, 2)
                    if before is not None:
                        residual(before, 1)
                    swap_pairs(b, 3)
                    maxima(b, 0)
                    swap_pairs(b, 4)
                    diagonals(b, 0)
                    maxima(b, 1)
                    swap_pairs(b, 5)

                def heads(b, more):
                    for h in range(HEADS):
                        if h + 1 < HEADS:
                            diagonals(b, h + 1)
                        turned_low(b, h)
                        if h + 2 < HEADS:
                            maxima(b, h + 2)
                        if h:
                            out_low(b, h - 1)
                        if h + AHEAD < HEADS:
                            swap_pairs(b, h + AHEAD)
                        if h == HEADS - 4 and more:
                            x_split(b + 1)
                    out_low(b, HEADS - 1)

                x_split(0)
                begin(0)
                with dve.Fori(0, BATCH - 1) as b:
                    heads(b, True)
                    begin(b + 1, b)
                heads(BATCH - 1, False)
                for m in range(HALVES):
                    residual(BATCH - 1, m)


def spill(nc, name, src, dst):
    with nc.semaphore(f"{name}_spilled") as spilled, nc.Block() as block:
        @block.sync
        def _(sp):
            sp.dma_start(dst, src[:]).then_inc(spilled, 16)
            sp.wait_ge(spilled, 16)


def route(nc, psum, norm, gates_t, a, ident):
    ctx, sb, sem = scopes(nc)
    with ctx:
        tiles = BATCH * TILES
        w = sb("router_w", [P, 2, EXPERTS])
        bias = sb("router_b", [P, EXPERTS])
        odds = sb("odds", [P, tiles, EXPERTS])
        top = sb("odds_top", [P, tiles])
        beats = sb("beats", [P, tiles, EXPERTS])
        rank = sb("rank", [P, tiles, EXPERTS])
        total = sb("odds_total", [P, tiles])
        params, cleared, logits_made, shifted, exp_made, step, gates_made, turned, kept = (
            sem(f"route_{n}") for n in ("params", "cleared", "logits_made", "shifted", "exp_made", "step",
                                        "gates_made", "turned", "kept"))
        logits = psum[:, 0, 0:tiles * EXPERTS].rearrange("p (t e) -> p t e", e=EXPERTS)
        wide = lambda x: x[:].rearrange("p (t o) -> p t o", o=1).broadcast_to((P, tiles, EXPERTS))
        with nc.Block() as block:
            @block.sync
            def _(sp):
                sp.dma_start(w[:], a["L0_ffn_router_w"].rearrange("(c p) e -> p c e", p=P)).then_inc(params, 16)
                sp.dma_start(bias[:], a["router_b"]).then_inc(params, 16)

            @block.tensor
            def _(pe):
                pe.wait_ge(params, 32)
                pe.wait_ge(cleared, 1)
                for t in range(tiles):
                    n, at = TILE_ROWS[t % TILES], TOK * (t // TILES) + P * (t % TILES)
                    for c in range(2):
                        last = pe.matmul(logits[0:n, t, :], norm[:, c, at:at + n], w[:, c, :],
                                         start=(c == 0), stop=(c == 1))
                last.then_inc(logits_made, 1)
                pe.wait_ge(gates_made, 1)
                for t in range(tiles):
                    n = TILE_ROWS[t % TILES]
                    last = pe.transpose(psum[0:EXPERTS, t // TILES, P * (t % TILES):P * (t % TILES) + n],
                                        odds[0:n, t, :], ident[0:n, 0:n])
                    if t % TILES == TILES - 1:
                        last.then_inc(turned, 1)

            @block.scalar
            def _(act):
                act.wait_ge(shifted, 1)
                act.activation(odds[:], odds[:], ACT.Exp).then_inc(exp_made, 1)
                for b in range(BATCH):
                    act.wait_ge(turned, b + 1)
                    act.activation(gates_t[:, tokens_of(b)], psum[0:EXPERTS, b, 0:TOK], ACT.Copy).then_inc(kept, 1)

            @block.vector
            def _(dve):
                done = [0]

                def link(ins):
                    done[0] += 1
                    ins.then_inc(step, 1)
                    dve.wait_ge(step, done[0])

                dve.memset(psum[:, 0, 0:tiles * EXPERTS], 0.0).then_inc(cleared, 1)
                for e in range(EXPERTS):
                    last = dve.memset(rank[:, :, e:e + 1], float(EXPERTS - 1 - e))
                link(last)
                dve.wait_ge(params, 32)
                dve.wait_ge(logits_made, 1)
                link(dve.tensor_tensor(odds[:], logits, bias[:].rearrange("p (o e) -> p o e", o=1)
                                       .broadcast_to((P, tiles, EXPERTS)), ALU.add))
                link(dve.tensor_reduce(top[:], odds[:], AX_X, ALU.max))
                dve.tensor_tensor(odds[:], odds[:], wide(top), ALU.subtract).then_inc(shifted, 1)
                dve.wait_ge(exp_made, 1)
                for d in range(1, EXPERTS):
                    k = EXPERTS - d
                    link(dve.tensor_tensor(beats[:, :, 0:k], odds[:, :, 0:k], odds[:, :, d:], ALU.is_ge))
                    link(dve.tensor_tensor(rank[:, :, 0:k], rank[:, :, 0:k], beats[:, :, 0:k], ALU.subtract))
                    link(dve.tensor_tensor(rank[:, :, d:], rank[:, :, d:], beats[:, :, 0:k], ALU.add))
                link(dve.tensor_scalar(rank[:], rank[:], 1.5, None, ALU.is_lt))
                link(dve.tensor_tensor(odds[:], odds[:], rank[:], ALU.mult))
                link(dve.tensor_reduce(total[:], odds[:], AX_X, ALU.add))
                link(dve.reciprocal(total[:], total[:]))
                dve.tensor_tensor(odds[:], odds[:], wide(total), ALU.mult).then_inc(gates_made, 1)


def split_norm(nc, norm, x):
    with nc.semaphore("norm_high") as high_made, nc.semaphore("norm_low") as low_made, nc.Block() as block:
        @block.scalar
        def _(act):
            with act.Fori(0, BATCH) as b:
                act.activation(x[0][:, :, tokens_of(b)], norm[:, :, tokens_of(b)], ACT.Copy).then_inc(high_made, 1)

        @block.vector
        def _(dve):
            with dve.Fori(0, BATCH) as b:
                dve.wait_ge(high_made, b + 1)
                dve.tensor_tensor(x[1][:, :, tokens_of(b)], norm[:, :, tokens_of(b)],
                                  x[0][:, :, tokens_of(b)].bitcast(F32), ALU.subtract).then_inc(low_made, 1)


EXPERT_COLS = 2 * 2 * FFN + FFN // P * DIM
SLICE = EXPERT_COLS // BATCH


def experts(nc, psum, hid, x, gates_t, a):
    ctx, sb, sem = scopes(nc)
    with ctx:
        chunks = FFN // P
        weights = [[sb(f"expert_w{i}_{part}", [P, EXPERT_COLS], F32R) for part in ("high", "low")] for i in range(2)]
        stage = sb("expert_stage", [P, SLICE])
        select = sb("expert_select", [EXPERTS, EXPERTS * P])
        silu = sb("silu", [P, 2, TOK])
        act_f = sb("expert_act", [P, 2, TOK])
        act_hl = [sb(f"expert_act_{part}", [P, 2, TOK], F32R) for part in ("high", "low")]
        gate = sb("gate", [P, 1, TOK])
        gated_out = sb("gated_out", [P, HALVES, TOK])
        three = ((0, 0), (0, 1), (1, 0))
        BANK_OUT, BANK_GATE = 4, 7

        def expert(e, run):
            now, coming = weights[e % 2], weights[(e + 1) % 2]
            fetch = e + 1 < EXPERTS
            with nc.Block() as block:
                (selected, w_in, w_high, w_low, up_made, silu_made, act_made, high_made, low_made, down_made,
                 gate_made, gate_kept, out_read, added) = sems

                @block.sync
                def _(sp):
                    if not run:
                        sp.dma_start(select[:], a["c_select"]).then_inc(selected, 16)
                    if fetch:
                        with sp.Fori(0, BATCH) as b:
                            sp.wait_ge(w_low, b + 1)
                            sp.dma_start(stage[:], a["experts"][e + 1, :, bass.ds(b * SLICE, SLICE)]).then_inc(w_in, 16)
                    if not run:
                        sp.wait_ge(selected, 16)

                def split_high(act, b):
                    act.wait_ge(w_in, 16 * b + 16)
                    act.activation(coming[0][:, bass.ds(b * SLICE, SLICE)], stage[:], ACT.Copy).then_inc(w_high, 1)

                @block.tensor
                def _(pe):
                    if not run:
                        return
                    pe.sem_inc(down_made, 2)
                    pe.sem_inc(gate_made, 1)

                    def up(b, f):
                        pe.wait_ge(act_made, chunks * b + f + 1)
                        t = tokens_of(b + f // chunks)
                        for k in range(2):
                            for i, (hw, hx) in enumerate(three):
                                for c in range(2):
                                    at = (2 * k + c) * FFN + P * (f % chunks)
                                    last = pe.matmul(psum[:, 2 * k + f % 2, 0:TOK], now[hw][:, at:at + P],
                                                     x[hx][:, c, t], start=(i == c == 0), stop=(i == 2 and c == 1))
                        last.then_inc(up_made, 1)

                    def down(b, f):
                        if f == 0:
                            pe.wait_ge(out_read, b + 1)
                        pe.wait_ge(low_made, chunks * b + f + 1 + 2)
                        for m in range(HALVES):
                            for i, (hw, hx) in enumerate(three):
                                at = 4 * FFN + DIM * f + P * m
                                last = pe.matmul(psum[:, BANK_OUT + m, 0:TOK], now[hw][:, at:at + P],
                                                 act_hl[hx][:, f % 2, :], start=(i == f == 0),
                                                 stop=(i == 2 and f == chunks - 1))
                        last.then_inc(down_made, 1)

                    def batch(b, ahead):
                        pe.wait_ge(gate_kept, b + 1)
                        pe.matmul(psum[:, BANK_GATE, 0:TOK], select[:, P * e:P * (e + 1)],
                                  gates_t[:, tokens_of(b)], start=True, stop=True).then_inc(gate_made, 1)
                        for f in range(chunks):
                            if f + 2 < chunks + ahead:
                                up(b, f + 2)
                            down(b, f)

                    up(0, 0)
                    up(0, 1)
                    with pe.Fori(0, BATCH - 1) as b:
                        batch(b, 2)
                    batch(BATCH - 1, 0)

                @block.scalar
                def _(act):
                    if not run:
                        with act.Fori(0, BATCH) as b:
                            split_high(act, b)
                        return
                    act.sem_inc(gate_kept, 1)
                    with act.Fori(0, BATCH) as b:
                        act.wait_ge(gate_made, b + 2)
                        act.wait_ge(out_read, b + 1)
                        act.activation(gate[:, 0, :], psum[:, BANK_GATE, 0:TOK], ACT.Copy).then_inc(gate_kept, 1)
                        for f in range(chunks):
                            act.wait_ge(up_made, chunks * b + f + 1)
                            act.activation(silu[:, f % 2, :], psum[:, f % 2, 0:TOK], ACT.Silu).then_inc(silu_made, 1)
                            act.wait_ge(act_made, chunks * b + f + 1 + 2)
                            act.wait_ge(down_made, chunks * b + f + 1)
                            act.activation(act_hl[0][:, f % 2, :], act_f[:, f % 2, :], ACT.Copy).then_inc(high_made, 1)
                        if fetch:
                            split_high(act, b)

                @block.vector
                def _(dve):
                    if not run:
                        return
                    dve.sem_inc(act_made, 2)
                    dve.sem_inc(out_read, 1)
                    with dve.Fori(0, BATCH) as b:
                        for f in range(chunks):
                            dve.wait_ge(silu_made, chunks * b + f + 1)
                            dve.wait_ge(low_made, chunks * b + f + 1)
                            dve.tensor_tensor(act_f[:, f % 2, :], psum[:, 2 + f % 2, 0:TOK], silu[:, f % 2, :],
                                              ALU.mult).then_inc(act_made, 1)
                        dve.wait_ge(gate_kept, b + 2)
                        dve.wait_ge(added, b + 1)
                        dve.wait_ge(down_made, chunks * b + chunks + 2)
                        dve.tensor_tensor(gated_out[:], psum[:, BANK_OUT:BANK_OUT + 2, 0:TOK],
                                          gate[:].broadcast_to((P, HALVES, TOK)), ALU.mult).then_inc(out_read, 1)

                @block.gpsimd
                def _(pool):
                    if fetch:
                        pool.sem_inc(w_low, 1)
                    if run:
                        pool.sem_inc(low_made, 2)
                        pool.sem_inc(added, 1)
                    with pool.Fori(0, BATCH) as b:
                        if run:
                            for f in range(chunks):
                                pool.wait_ge(high_made, chunks * b + f + 1)
                                pool.tensor_tensor(act_hl[1][:, f % 2, :], act_f[:, f % 2, :],
                                                   act_hl[0][:, f % 2, :].bitcast(F32),
                                                   ALU.subtract).then_inc(low_made, 1)
                        if fetch:
                            pool.wait_ge(w_high, b + 1)
                            cols = bass.ds(b * SLICE, SLICE)
                            pool.tensor_tensor(coming[1][:, cols], stage[:], coming[0][:, cols].bitcast(F32),
                                               ALU.subtract).then_inc(w_low, 1)
                        if run:
                            pool.wait_ge(out_read, b + 2)
                            t = tokens_of(b)
                            pool.tensor_tensor(hid[:, :, t], hid[:, :, t], gated_out[:], ALU.add).then_inc(added, 1)

        sems = [sem(f"expert_{n}") for n in
                ("selected", "w_in", "w_high", "w_low", "up_made", "silu_made", "act_made", "high_made",
                 "low_made", "down_made", "gate_made", "gate_kept", "out_read", "added")]
        expert(-1, False)
        for e in range(EXPERTS):
            clear(nc, sems)
            expert(e, True)


def recurrence_tables(nc, vec, consts, turn, feed, decay):
    ctx, sb, sem = scopes(nc)
    with ctx:
        col = {n: sb(f"rec_{n}", [P, HALVES]) for n in
               ("square", "other", "size", "zero", "inv", "re", "im", "norm2", "root", "unit", "fix")}
        tmp = sb("rec_tmp", [P, 2, TOK])
        step, decayed, rooted = sem("rec_step"), sem("rec_decayed"), sem("rec_rooted")
        re, im = vec["L1_attn_phazor_real"], vec["L1_attn_phazor_imag"]
        pr, pi = vec["L1_attn_phazor_init_real"], vec["L1_attn_phazor_init_imag"]
        with nc.Block() as block:
            @block.scalar
            def _(act):
                act.wait_ge(step, 3)
                act.activation(decay[:], col["square"][:], ACT.Exp, scale=-1.0).then_inc(decayed, 1)
                act.wait_ge(step, STEPS_TO_NORM)
                act.activation(col["root"][:], col["norm2"][:], ACT.Sqrt).then_inc(rooted, 1)

            @block.vector
            def _(dve):
                done = [0]

                def link(ins):
                    done[0] += 1
                    ins.then_inc(step, 1)
                    dve.wait_ge(step, done[0])

                c = {n: t[:] for n, t in col.items()}
                tt = lambda o, x, y, op: link(dve.tensor_tensor(o, x, y, op))
                tt(c["square"], re, re, ALU.mult)
                tt(c["other"], im, im, ALU.mult)
                tt(c["square"], c["square"], c["other"], ALU.add)
                link(dve.tensor_scalar(c["size"], re, -1.0, None, ALU.mult))
                tt(c["size"], c["size"], re, ALU.max)
                tt(c["size"], c["size"], im, ALU.max)
                link(dve.tensor_scalar(c["other"], im, -1.0, None, ALU.mult))
                tt(c["size"], c["size"], c["other"], ALU.max)
                link(dve.tensor_scalar(c["zero"], c["size"], 0.0, None, ALU.is_equal))
                tt(c["size"], c["size"], c["zero"], ALU.add)
                link(dve.reciprocal(c["inv"], c["size"]))
                tt(c["re"], re, c["inv"], ALU.mult)
                tt(c["re"], c["re"], c["zero"], ALU.add)
                tt(c["im"], im, c["inv"], ALU.mult)
                tt(c["norm2"], c["re"], c["re"], ALU.mult)
                tt(c["other"], c["im"], c["im"], ALU.mult)
                tt(c["norm2"], c["norm2"], c["other"], ALU.add)
                assert done[0] == STEPS_TO_NORM
                dve.wait_ge(rooted, 1)
                link(dve.reciprocal(c["unit"], c["root"]))
                for _ in range(2):
                    tt(c["fix"], c["unit"], c["unit"], ALU.mult)
                    tt(c["fix"], c["fix"], c["norm2"], ALU.mult)
                    link(dve.tensor_scalar(c["fix"], c["fix"], -0.5, 1.5, ALU.mult, ALU.add))
                    tt(c["unit"], c["unit"], c["fix"], ALU.mult)
                for part, x in enumerate(("re", "im")):
                    last = dve.tensor_tensor(turn[:, part, :, 0], c[x], c["unit"], ALU.mult)
                link(last)
                n = 1
                while n < TOK:
                    k = min(n, TOK - n)
                    for h in range(HALVES):
                        for part in range(2):
                            last = dve.tensor_scalar(tmp[:, part, 0:k], turn[:, 1 - part, h, 0:k],
                                                     turn[:, 1, h, n - 1:n], None, ALU.mult)
                        link(last)
                        for part, op in ((0, ALU.subtract), (1, ALU.add)):
                            last = dve.scalar_tensor_tensor(turn[:, part, h, n:n + k], turn[:, part, h, 0:k],
                                                            turn[:, 0, h, n - 1:n], tmp[:, part, 0:k], ALU.mult, op)
                        link(last)
                    n += k
                for h in range(HALVES):
                    for part, x in enumerate((pi, pr)):
                        last = dve.tensor_scalar(tmp[:, part, :], turn[:, 1, h, :], x[:, h:h + 1], None, ALU.mult)
                    link(last)
                    for part, (x, op) in enumerate(((pr, ALU.add), (pi, ALU.subtract))):
                        last = dve.scalar_tensor_tensor(feed[:, part, h, :], turn[:, 0, h, :], x[:, h:h + 1],
                                                        tmp[:, part, :], ALU.mult, op)
                    link(last)
                dve.wait_ge(decayed, 1)


STEPS_TO_NORM = 17


def recurrence(nc, norm, hid, vec, turn, feed, decay):
    ctx, sb, sem = scopes(nc)
    with ctx:
        fed = sb("fed", [P, 2, 2, HALVES, TOK])
        state = sb("state", [P, 2, 2, HALVES, TOK])
        fed_made, scanned, im_made, re_made, joined, added = (
            sem(f"rec_{n}") for n in ("fed_made", "scanned", "im_made", "re_made", "joined", "added"))
        last_parts = (vec["L1_attn_last_conv_real"], vec["L1_attn_last_conv_imag"])
        with nc.Block() as block:
            @block.gpsimd
            def _(pool):
                with pool.Fori(0, BATCH // 2) as i:
                    for u in range(2):
                        t = tokens_of(2 * i + u)
                        pool.wait_ge(joined, 2 * i + u + 1)
                        for part in range(2):
                            last = pool.tensor_tensor(fed[:, u, part, :, :], norm[:, :, t], feed[:, part, :, :], ALU.mult)
                        last.then_inc(fed_made, 1)
                    for u in range(2):
                        pool.wait_ge(scanned, 2 * i + u + 1)
                        pool.tensor_tensor(state[:, u, 1, :, :], state[:, u, 1, :, :], turn[:, 1, :, :],
                                           ALU.mult).then_inc(im_made, 1)

            @block.vector
            def _(dve):
                dve.sem_inc(joined, 2)
                with dve.Fori(0, BATCH // 2) as i:
                    for u in range(2):
                        dve.wait_ge(fed_made, 2 * i + u + 1)
                        for part in range(2):
                            for h in range(HALVES):
                                last = dve.tensor_tensor_scan(state[:, u, part, h, :],
                                                              decay[:, h:h + 1].broadcast_to((P, TOK)),
                                                              fed[:, u, part, h, :], last_parts[part][:, h:h + 1],
                                                              ALU.mult, ALU.add)
                        last.then_inc(scanned, 1)
                    for u in range(2):
                        t = tokens_of(2 * i + u)
                        dve.wait_ge(scanned, 2 * i + u + 1)
                        dve.tensor_tensor(state[:, u, 0, :, :], state[:, u, 0, :, :], turn[:, 0, :, :],
                                          ALU.mult).then_inc(re_made, 1)
                        dve.wait_ge(re_made, 2 * i + u + 1)
                        dve.tensor_tensor(hid[:, :, t], hid[:, :, t], state[:, u, 0, :, :], ALU.add).then_inc(added, 1)
                        dve.wait_ge(im_made, 2 * i + u + 1)
                        dve.wait_ge(added, 2 * i + u + 1)
                        dve.tensor_tensor(hid[:, :, t], hid[:, :, t], state[:, u, 1, :, :],
                                          ALU.subtract).then_inc(joined, 1)


MAGIC = 1.5 * 2.0 ** 23
ACT_MAX = 32767.0
WEIGHT_MAX = 7.0
SIG_STEPS = 65536.0
TINY = 1e-12
QCHUNKS = QFFN // P
QCOLS = QFFN * DIM // P
RMAX = bass.bass_isa.ReduceOp.max


def quantised_weights(nc, psum, a, ident, up_gate, down):
    ctx, sb, sem = scopes(nc)
    with ctx:
        w = sb("q_raw", [P, 3 * QCOLS])
        scale = sb("q_scale", [P, 3 * QCOLS // QBLOCK])
        inv = sb("q_inv", [P, 3 * QCOLS // QBLOCK])
        w_in, step, made, turned, high_made, low_made = (
            sem(f"q_{n}") for n in ("w_in", "step", "made", "turned", "high_made", "low_made"))
        blocks = w[:].rearrange("p (n k) -> p n k", k=QBLOCK)
        per_block = lambda x: x[:].rearrange("p (n o) -> p n o", o=1).broadcast_to((P, 3 * QCOLS // QBLOCK, QBLOCK))
        groups = []
        for m in range(2):
            for c in range(HALVES):
                for g in range(0, QCHUNKS, 3):
                    groups.append((m * QCOLS + g * DIM + c * P, DIM,
                                   [up_gate[k][:, c, m * QFFN + g * P:m * QFFN + (g + 3) * P] for k in range(2)]))
        for m in range(HALVES):
            for g in range(0, QCHUNKS, 3):
                groups.append((2 * QCOLS + m * QFFN + g * P, P,
                               [down[k][:, g:g + 3, m * P:(m + 1) * P] for k in range(2)]))

        def group_bank(n, like):
            x = psum[:, n % 8, 0:3 * P]
            return x if len(like.shape) == 2 else x.rearrange("p (k n) -> p k n", k=3)

        with nc.Block() as block:
            @block.sync
            def _(sp):
                for i, name in enumerate(("L1_ffn_w_up", "L1_ffn_w_gate")):
                    sp.dma_start(w[:, i * QCOLS:(i + 1) * QCOLS].rearrange("p (t n) -> p t n", n=DIM),
                                 a[name].rearrange("(t p) n -> p t n", p=P)).then_inc(w_in, 16)
                sp.dma_start(w[:, 2 * QCOLS:].rearrange("p (t n) -> p t n", n=QFFN),
                             a["L1_ffn_w_down"].rearrange("(t p) n -> p t n", p=P)).then_inc(w_in, 16)

            @block.vector
            def _(dve):
                done = [0]

                def link(ins):
                    done[0] += 1
                    ins.then_inc(step, 1)
                    dve.wait_ge(step, done[0])

                dve.wait_ge(w_in, 48)
                link(dve.tensor_reduce(scale[:], blocks, AX_X, ALU.max, apply_absolute_value=True))
                link(dve.tensor_scalar(scale[:], scale[:], 1.0 / WEIGHT_MAX, TINY, ALU.mult, ALU.max))
                link(dve.reciprocal(inv[:], scale[:]))
                link(dve.tensor_tensor(blocks, blocks, per_block(inv), ALU.mult))
                link(dve.tensor_scalar(w[:], w[:], MAGIC, MAGIC, ALU.add, ALU.subtract))
                dve.tensor_tensor(blocks, blocks, per_block(scale), ALU.mult).then_inc(made, 1)
                for n, (_, _, dst) in enumerate(groups):
                    dve.wait_ge(high_made, n + 1)
                    dve.tensor_tensor(dst[1], group_bank(n, dst[1]), dst[0].bitcast(F32),
                                      ALU.subtract).then_inc(low_made, 1)

            @block.tensor
            def _(pe):
                pe.wait_ge(made, 1)
                for n, (at, apart, _) in enumerate(groups):
                    if n >= 8:
                        pe.wait_ge(low_made, n - 7)
                    for k in range(3):
                        last = pe.transpose(psum[:, n % 8, P * k:P * (k + 1)],
                                            w[:, at + apart * k:at + apart * k + P], ident[:])
                    last.then_inc(turned, 1)

            @block.scalar
            def _(act):
                for n, (_, _, dst) in enumerate(groups):
                    act.wait_ge(turned, n + 1)
                    act.activation(dst[0], group_bank(n, dst[0]), ACT.Copy).then_inc(high_made, 1)


def absolute_max(nc, peaks, x):
    with nc.Block() as block:
        @block.vector
        def _(dve):
            with dve.Fori(0, BATCH) as b:
                dve.tensor_reduce(peaks[:, bass.ds(b, 1)], x[:, :, tokens_of(b)], AX_XY, ALU.max, apply_absolute_value=True)


def step_size(nc, name, peaks, scale, inv, times=None):
    ctx, sb, sem = scopes(nc)
    with ctx:
        own = sb(f"{name}_own", [P, 1])
        peak = sb(f"{name}_peak", [P, 1])
        owned, shared, step = sem(f"{name}_owned"), sem(f"{name}_shared"), sem(f"{name}_step")
        with nc.Block() as block:
            @block.gpsimd
            def _(pool):
                pool.wait_ge(owned, 1)
                pool.partition_all_reduce(peak[:], own[:], P, RMAX).then_inc(shared, 1)

            @block.vector
            def _(dve):
                dve.tensor_reduce(own[:], peaks[:], AX_X, ALU.max).then_inc(owned, 1)
                dve.wait_ge(shared, 1)
                n = 0
                if times is not None:
                    dve.tensor_tensor(peak[:], peak[:], times, ALU.mult).then_inc(step, 1)
                    n = 1
                    dve.wait_ge(step, n)
                dve.tensor_scalar(scale, peak[:], 1.0 / ACT_MAX, TINY, ALU.mult, ALU.max).then_inc(step, 1)
                dve.wait_ge(step, n + 1)
                dve.reciprocal(inv, scale).then_inc(step, 1)
                if times is not None:
                    dve.wait_ge(step, n + 2)
                    dve.tensor_tensor(inv, inv, times, ALU.mult)


def quantised_ffn(nc, psum, norm, hid, a, consts, up_gate, down, out):
    ctx, sb, sem = scopes(nc)
    up_dram = nc.dram_tensor("up_spill", [P, QCHUNKS, TOKENS], F32, kind="Internal").ap()
    three = ((0, 0), (0, 1), (1, 0))
    with ctx:
        gate = sb("q_gate", [P, QCHUNKS, TOKENS])
        peaks = sb("q_peaks", [P, 4, BATCH])
        steps = sb("q_steps", [P, 12])
        (S_X, I_X, S_UP, I_UP, S_GATE, I_GATE, S_ACT, I_ACT, S_BOTH, S_OUT, I_OUT) = (
            steps[:, i:i + 1] for i in range(11))
        magic, minus_magic = consts[:, PLUS_MAGIC:PLUS_MAGIC + 1], consts[:, MINUS_MAGIC:MINUS_MAGIC + 1]
        X_, UP_, GATE_, OUT_ = range(4)
        two = BATCH // 2

        absolute_max(nc, peaks[:, X_, :], norm)
        step_size(nc, "q_x", peaks[:, X_, :], S_X, I_X)

        with ExitStack() as part:
            q = part.enter_context(nc.sbuf_tensor("q_tokens", [P, 2, HALVES, TOK], F32))
            qhl = [part.enter_context(nc.sbuf_tensor(f"q_tokens_{k}", [P, 2, HALVES, TOK], F32R)) for k in ("high", "low")]
            up = part.enter_context(nc.sbuf_tensor("q_up", [P, QCHUNKS, TOK], F32))
            q_made, high_made, low_made, made, kept, up_out, peak_made = (
                part.enter_context(nc.semaphore(f"q1_{n}")) for n in
                ("q_made", "high_made", "low_made", "made", "kept", "up_out", "peak_made"))
            block = part.enter_context(nc.Block())
            BANKS = 6

            @block.vector
            def _(dve):
                dve.sem_inc(peak_made, 2)

                def rounded(n, u):
                    dve.tensor_scalar(q[:, u, :, :], norm[:, :, tokens_of(n)], I_X, MAGIC,
                                      ALU.mult, ALU.add).then_inc(q_made, 1)
                    dve.wait_ge(high_made, n + 1)
                    dve.scalar_tensor_tensor(qhl[1][:, u, :, :], q[:, u, :, :], MAGIC,
                                             qhl[0][:, u, :, :].bitcast(F32), ALU.subtract,
                                             ALU.subtract).then_inc(low_made, 1)

                with dve.Fori(0, two) as i:
                    for u in range(2):
                        n = 2 * i + u
                        rounded(n, u)
                        dve.wait_ge(kept, 12 * n + 6 + BANKS)
                        dve.tensor_reduce(peaks[:, UP_, bass.ds(n, 1)], up[:], AX_XY, ALU.max,
                                          apply_absolute_value=True).then_inc(peak_made, 1)
                        dve.wait_ge(kept, 12 * n + 12 + BANKS)
                        dve.tensor_reduce(peaks[:, GATE_, bass.ds(n, 1)], gate[:, :, tokens_of(n)], AX_XY, ALU.max,
                                          apply_absolute_value=True)

            @block.scalar
            def _(act):
                act.sem_inc(kept, BANKS)
                act.sem_inc(up_out, 16)
                with act.Fori(0, two) as i:
                    for u in range(2):
                        n = 2 * i + u
                        act.wait_ge(q_made, n + 1)
                        act.activation(qhl[0][:, u, :, :], q[:, u, :, :], ACT.Identity,
                                       bias=minus_magic).then_inc(high_made, 1)
                        for j in range(2 * QCHUNKS):
                            act.wait_ge(made, 12 * n + j + 1)
                            if j == 0:
                                act.wait_ge(up_out, 16 * n + 16)
                                act.wait_ge(peak_made, n + 2)
                            dst = up[:, j, :] if j < QCHUNKS else gate[:, j - QCHUNKS, tokens_of(n)]
                            act.activation(dst, psum[:, j % BANKS, 0:TOK], ACT.Copy, scale=S_X).then_inc(kept, 1)

            @block.tensor
            def _(pe):
                with pe.Fori(0, two) as i:
                    for u in range(2):
                        n = 2 * i + u
                        pe.wait_ge(low_made, n + 1)
                        for j in range(2 * QCHUNKS):
                            pe.wait_ge(kept, 12 * n + j + 1)
                            for k, (hw, hx) in enumerate(three):
                                for c in range(HALVES):
                                    last = pe.matmul(psum[:, j % BANKS, 0:TOK], up_gate[hw][:, c, P * j:P * (j + 1)],
                                                     qhl[hx][:, u, c, :], start=(k == c == 0), stop=(k == 2 and c == 1))
                            last.then_inc(made, 1)

            @block.sync
            def _(sp):
                with sp.Fori(0, BATCH) as n:
                    sp.wait_ge(kept, 12 * n + 6 + BANKS)
                    sp.dma_start(up_dram[:, :, tokens_of(n)], up[:]).then_inc(up_out, 16)
                sp.wait_ge(up_out, 16 * BATCH + 16)

        step_size(nc, "q_up", peaks[:, UP_, :], S_UP, I_UP)
        step_size(nc, "q_gate", peaks[:, GATE_, :], S_GATE, I_GATE)

        with ExitStack() as part:
            sig = part.enter_context(nc.sbuf_tensor("q_sig", [P, 2, QCHUNKS, TOK], F32))
            scaled, rounded, sig_made, sig_scaled, sig_ready, prod_made = (
                part.enter_context(nc.semaphore(f"q2_{n}")) for n in
                ("scaled", "rounded", "sig_made", "sig_scaled", "sig_ready", "prod_made"))
            block = part.enter_context(nc.Block())

            @block.vector
            def _(dve):
                def front(n):
                    g = gate[:, :, tokens_of(n)]
                    dve.tensor_scalar(g, g, I_GATE, MAGIC, ALU.mult, ALU.add).then_inc(scaled, 1)
                    dve.wait_ge(scaled, n + 1)
                    dve.tensor_scalar(g, g, MAGIC, S_GATE, ALU.subtract, ALU.mult).then_inc(rounded, 1)

                def back(n, u):
                    dve.wait_ge(sig_scaled, n + 1)
                    dve.tensor_scalar(sig[:, u, :, :], sig[:, u, :, :], MAGIC + SIG_STEPS - 1, MAGIC,
                                      ALU.min, ALU.subtract).then_inc(sig_ready, 1)

                def peak(n):
                    dve.wait_ge(prod_made, n + 1 + 2)
                    dve.tensor_reduce(peaks[:, X_, bass.ds(n, 1)], gate[:, :, tokens_of(n)], AX_XY, ALU.max,
                                      apply_absolute_value=True)

                with dve.Fori(0, two) as i:
                    front(2 * i)
                    front(2 * i + 1)
                    back(2 * i, 0)
                    back(2 * i + 1, 1)
                    peak(2 * i)
                    peak(2 * i + 1)

            @block.scalar
            def _(act):
                with act.Fori(0, two) as i:
                    for u in range(2):
                        n = 2 * i + u
                        act.wait_ge(rounded, n + 1)
                        act.wait_ge(prod_made, n + 1)
                        act.activation(sig[:, u, :, :], gate[:, :, tokens_of(n)], ACT.Sigmoid).then_inc(sig_made, 1)
                        act.wait_ge(sig_made, n + 1)
                        act.activation(sig[:, u, :, :], sig[:, u, :, :], ACT.Identity, scale=SIG_STEPS,
                                       bias=magic).then_inc(sig_scaled, 1)

            @block.gpsimd
            def _(pool):
                pool.sem_inc(prod_made, 2)
                with pool.Fori(0, two) as i:
                    for u in range(2):
                        n = 2 * i + u
                        pool.wait_ge(sig_ready, n + 1)
                        g = gate[:, :, tokens_of(n)]
                        pool.tensor_tensor(g, g, sig[:, u, :, :], ALU.mult).then_inc(prod_made, 1)

        step_size(nc, "q_act", peaks[:, X_, :], S_ACT, I_ACT)

        with ExitStack() as part:
            up = part.enter_context(nc.sbuf_tensor("q_up2", [P, 2, QCHUNKS, TOK], F32))
            up_in = [part.enter_context(nc.semaphore(f"q3_up_in{u}")) for u in range(2)]
            act_scaled, up_scaled, up_rounded, prod_made = (
                part.enter_context(nc.semaphore(f"q3_{n}")) for n in
                ("act_scaled", "up_scaled", "up_rounded", "prod_made"))
            block = part.enter_context(nc.Block())

            @block.sync
            def _(sp):
                with sp.Fori(0, two) as i:
                    for u in range(2):
                        sp.wait_ge(prod_made, 2 * i + u + 1)
                        sp.dma_start(up[:, u, :, :], up_dram[:, :, tokens_of(2 * i + u)]).then_inc(up_in[u], 16)

            @block.scalar
            def _(act):
                with act.Fori(0, two) as i:
                    for u in range(2):
                        n = 2 * i + u
                        g = gate[:, :, tokens_of(n)]
                        act.activation(g, g, ACT.Identity, scale=I_ACT, bias=magic).then_inc(act_scaled, 1)
                        act.wait_ge(up_scaled, n + 1)
                        act.activation(up[:, u, :, :], up[:, u, :, :], ACT.Identity,
                                       bias=minus_magic).then_inc(up_rounded, 1)

            @block.vector
            def _(dve):
                dve.sem_inc(prod_made, 2)
                dve.tensor_scalar(S_BOTH, S_ACT, S_UP, 1.0 / SIG_STEPS, ALU.mult, ALU.mult)
                with dve.Fori(0, two) as i:
                    for u in range(2):
                        dve.wait_ge(up_in[u], 16 * i + 16)
                        dve.tensor_scalar(up[:, u, :, :], up[:, u, :, :], I_UP, MAGIC,
                                          ALU.mult, ALU.add).then_inc(up_scaled, 1)
                    for u in range(2):
                        n = 2 * i + u
                        dve.wait_ge(act_scaled, n + 1)
                        dve.wait_ge(up_rounded, n + 1)
                        g = gate[:, :, tokens_of(n)]
                        dve.scalar_tensor_tensor(g, g, MAGIC, up[:, u, :, :], ALU.subtract,
                                                 ALU.mult).then_inc(prod_made, 1)
                        dve.wait_ge(prod_made, n + 1 + 2)
                        dve.tensor_reduce(peaks[:, OUT_, bass.ds(n, 1)], g, AX_XY, ALU.max, apply_absolute_value=True)

        step_size(nc, "q_out", peaks[:, OUT_, :], S_OUT, I_OUT, times=S_BOTH)

        with ExitStack() as part:
            q = part.enter_context(nc.sbuf_tensor("q_prod", [P, QCHUNKS, TOK], F32))
            qhl = [part.enter_context(nc.sbuf_tensor(f"q_prod_{k}", [P, QCHUNKS, TOK], F32R)) for k in ("high", "low")]
            result = part.enter_context(nc.sbuf_tensor("result", [P, 2, HALVES, TOK], F32))
            stored = [part.enter_context(nc.semaphore(f"q4_stored{u}")) for u in range(2)]
            q_made, high_made, low_made, made, result_made = (
                part.enter_context(nc.semaphore(f"q4_{n}")) for n in
                ("q_made", "high_made", "low_made", "made", "result_made"))
            block = part.enter_context(nc.Block())

            @block.vector
            def _(dve):
                dve.sem_inc(low_made, 1)
                dve.sem_inc(result_made, 2)
                with dve.Fori(0, two) as i:
                    for u in range(2):
                        n = 2 * i + u
                        dve.tensor_scalar(q[:], gate[:, :, tokens_of(n)], I_OUT, MAGIC,
                                          ALU.mult, ALU.add).then_inc(q_made, 1)
                        dve.wait_ge(high_made, n + 1)
                        dve.scalar_tensor_tensor(qhl[1][:], q[:], MAGIC, qhl[0][:].bitcast(F32), ALU.subtract,
                                                 ALU.subtract).then_inc(low_made, 1)
                        dve.wait_ge(made, n + 1 + 1)
                        dve.wait_ge(stored[u], 16 * i + 16)
                        dve.scalar_tensor_tensor(result[:, u, :, :], psum[:, 2 * u:2 * u + 2, 0:TOK], S_OUT,
                                                 hid[:, :, tokens_of(n)], ALU.mult, ALU.add).then_inc(result_made, 1)

            @block.scalar
            def _(act):
                with act.Fori(0, two) as i:
                    for u in range(2):
                        n = 2 * i + u
                        act.wait_ge(q_made, n + 1)
                        act.wait_ge(made, n + 1)
                        act.activation(qhl[0][:], q[:], ACT.Identity, bias=minus_magic).then_inc(high_made, 1)

            @block.tensor
            def _(pe):
                pe.sem_inc(made, 1)
                with pe.Fori(0, two) as i:
                    for u in range(2):
                        n = 2 * i + u
                        pe.wait_ge(low_made, n + 1 + 1)
                        pe.wait_ge(result_made, n + 1)
                        for m in range(HALVES):
                            for k, (hw, hx) in enumerate(three):
                                for c in range(QCHUNKS):
                                    last = pe.matmul(psum[:, 2 * u + m, 0:TOK], down[hw][:, c, P * m:P * (m + 1)],
                                                     qhl[hx][:, c, :], start=(k == c == 0),
                                                     stop=(k == 2 and c == QCHUNKS - 1))
                        last.then_inc(made, 1)

            @block.sync
            def _(sp):
                for u in range(2):
                    sp.sem_inc(stored[u], 16)
                with sp.Fori(0, two) as i:
                    for u in range(2):
                        n = 2 * i + u
                        sp.wait_ge(result_made, n + 1 + 2)
                        sp.dma_start(out[:, :, tokens_of(n)], result[:, u, :, :]).then_inc(stored[u], 16)
                for u in range(2):
                    sp.wait_ge(stored[u], 16 * two + 16)


def audio_tower(nc, a, out, stop=None, dump=None):
    with ExitStack() as ctx:
        psum = ctx.enter_context(nc.psum_tensor("psum", [P, 8, BANK], F32))
        hid_dram = nc.dram_tensor("hid_spill", [P, HALVES, TOKENS], F32, kind="Internal").ap()
        norm = ctx.enter_context(nc.sbuf_tensor("norm", [P, HALVES, TOKENS], F32))
        consts = ctx.enter_context(nc.sbuf_tensor("consts", [P, 4], F32))
        ones = ctx.enter_context(nc.sbuf_tensor("ones", [P, P], F32))
        ident = ctx.enter_context(nc.sbuf_tensor("ident", [P, P], F32))
        vectors = ctx.enter_context(nc.sbuf_tensor("vectors", [P, len(VECTORS), HALVES], F32))
        vec = {name: vectors[:, i, :] for i, name in enumerate(VECTORS)}
        ln_sems = [ctx.enter_context(nc.semaphore(f"ln_{n}")) for n in
                   ("mean_made", "centered", "squared", "var_made", "std_made", "rstd_made", "normed")]
        const_in = ctx.enter_context(nc.semaphore("const_in"))
        with nc.Block() as block:
            @block.sync
            def _(sp):
                sp.dma_start(consts[:], a["c_columns"]).then_inc(const_in, 16)
                sp.dma_start(ident[:], a["c_ident"]).then_inc(const_in, 16)
                sp.dma_start(vectors[:], a["vectors"]).then_inc(const_in, 16)
                sp.wait_ge(const_in, 48)

            @block.vector
            def _(dve):
                dve.memset(ones[:], 1.0 / DIM)

        with nc.sbuf_tensor("hid", [P, HALVES, TOKENS], F32) as hid:
            tokenize(nc, psum, hid, a["patches"], a["L0_tok_W"], vec["L0_tok_b"])
            layernorm(nc, psum, ln_sems, "ln_tok", hid, hid, consts, ones, EPS_TOK,
                      (vec["L0_tok_gamma"], vec["L0_tok_beta"]))
            spill(nc, "tok", hid, hid_dram)
            layernorm(nc, psum, ln_sems, "ln_attn", hid, norm, consts, ones, EPS_LN)
        attention(nc, psum, norm, hid_dram, a, consts, ident, vec["L0_attn_bo"])
        if stop == "attn":
            return dump(nc, norm, norm)
        with ExitStack() as moe:
            gates_t = moe.enter_context(nc.sbuf_tensor("gates_t", [EXPERTS, TOKENS], F32))
            x = [moe.enter_context(nc.sbuf_tensor(f"xm_{part}", [P, HALVES, TOKENS], F32R)) for part in ("high", "low")]
            with nc.sbuf_tensor("norm2", [P, HALVES, TOKENS], F32) as norm2:
                layernorm(nc, psum, ln_sems, "ln_ffn", norm, norm2, consts, ones, EPS_LN)
                route(nc, psum, norm2, gates_t, a, ident)
                split_norm(nc, norm2, x)
            experts(nc, psum, norm, x, gates_t, a)
        if stop == "moe":
            return dump(nc, norm, norm)
        hid = norm
        with ExitStack() as rec:
            norm3 = rec.enter_context(nc.sbuf_tensor("norm3", [P, HALVES, TOKENS], F32))
            turn = rec.enter_context(nc.sbuf_tensor("turn", [P, 2, HALVES, TOK], F32))
            feed = rec.enter_context(nc.sbuf_tensor("feed", [P, 2, HALVES, TOK], F32))
            decay = rec.enter_context(nc.sbuf_tensor("decay", [P, HALVES], F32))
            recurrence_tables(nc, vec, consts, turn, feed, decay)
            layernorm(nc, psum, ln_sems, "ln_rec", hid, norm3, consts, ones, EPS_LN)
            recurrence(nc, norm3, hid, vec, turn, feed, decay)
        if stop == "conv":
            return dump(nc, hid, hid)
        up_gate = [ctx.enter_context(nc.sbuf_tensor(f"up_gate_{part}", [P, HALVES, 2 * QFFN], F32R))
                   for part in ("high", "low")]
        down = [ctx.enter_context(nc.sbuf_tensor(f"down_{part}", [P, QCHUNKS, DIM], F32R))
                for part in ("high", "low")]
        quantised_weights(nc, psum, a, ident, up_gate, down)
        with nc.sbuf_tensor("norm4", [P, HALVES, TOKENS], F32) as norm4:
            layernorm(nc, psum, ln_sems, "ln_q", hid, norm4, consts, ones, EPS_LN)
            quantised_ffn(nc, psum, norm4, hid, a, consts, up_gate, down, out)


def constants():
    columns = np.zeros((P, 4), np.float32)
    columns[:, EPS_TOK] = 1e-6
    columns[:, EPS_LN] = 1e-5
    columns[:, PLUS_MAGIC] = MAGIC
    columns[:, MINUS_MAGIC] = -MAGIC
    inv_freq = np.float32(1.0) / np.float32(10000.0) ** (np.arange(0, HEAD, 2, dtype=np.float32) / np.float32(HEAD))
    angle = np.arange(TOK, dtype=np.float32)[:, None] * inv_freq[None, :]
    pair = (np.arange(P) % HEAD) // 2
    sign = np.where(np.arange(P) % 2 == 0, -1.0, 1.0).astype(np.float32)[:, None]
    scale = np.array([HEAD ** -0.5, 1.0], np.float32)[None, :, None]
    cos = np.cos(angle).astype(np.float32).T[pair][:, None, :] * scale
    sin = (np.sin(angle).astype(np.float32).T[pair] * sign)[:, None, :] * scale
    behind = np.arange(P)[None, :] > np.arange(P)[:, None]
    select = np.repeat(np.eye(EXPERTS, dtype=np.float32), P, axis=1)
    return {"c_select": select, "c_cos": cos, "c_sin": sin, "c_mask": np.where(behind, NEG, 0.0).astype(np.float32),
            "c_columns": columns, "c_ident": np.eye(P, dtype=np.float32)}


def lay_out(inputs):
    x = np.asarray(inputs["x"])
    padded = np.zeros((BATCH, TOK // (FREQ // PATCH) * PATCH, FREQ), np.float32)
    padded[:, :TIME] = x
    p = padded.reshape(BATCH, -1, PATCH, FREQ // PATCH, PATCH).transpose(2, 4, 0, 1, 3)
    a = {"patches": np.ascontiguousarray(p.reshape(2, P, TOKENS).transpose(1, 0, 2))}
    v = np.stack([np.asarray(inputs[name]) for name in VECTORS])
    a["vectors"] = np.ascontiguousarray(v.reshape(len(VECTORS), HALVES, P).transpose(2, 0, 1))
    w13 = np.concatenate([np.asarray(inputs[n]).reshape(EXPERTS, 2, P, FFN).transpose(0, 2, 1, 3).reshape(EXPERTS, P, -1)
                          for n in ("L0_ffn_w1", "L0_ffn_w3")], axis=2)
    w2 = np.asarray(inputs["L0_ffn_w2"]).reshape(EXPERTS, FFN // P, P, DIM).transpose(0, 2, 1, 3).reshape(EXPERTS, P, -1)
    a["experts"] = np.concatenate([w13, w2], axis=2)
    a["router_b"] = np.tile(np.asarray(inputs["L0_ffn_router_b"]), (P, 1))
    moved = ("x", "L0_ffn_w1", "L0_ffn_w3", "L0_ffn_w2", "L0_ffn_router_b")
    for name, v in inputs.items():
        if name not in moved and name not in VECTORS:
            a[name] = np.ascontiguousarray(np.asarray(v))
    return a


def kernel(**inputs):
    import concourse.bacc as bacc
    from concourse.bass_utils import run_bass_kernel_spmd

    nc = bacc.Bacc("TRN2", target_bir_lowering=False, num_devices=1)
    arrays = {f"in_{name}": v for name, v in {**lay_out(inputs), **constants()}.items()}
    args = {name: nc.dram_tensor(name, v.shape, mybir.dt.from_np(v.dtype), kind="ExternalInput").ap()
            for name, v in arrays.items()}
    out = nc.dram_tensor("out_features", (P, HALVES, TOKENS), F32, kind="ExternalOutput").ap()
    audio_tower(nc, {name[3:]: v for name, v in args.items()}, out)
    got = run_bass_kernel_spmd(nc, [arrays], core_ids=[0]).results[0]["out_features"]
    return np.ascontiguousarray(got.transpose(2, 1, 0).reshape(BATCH, TOK, DIM))
```

```python
from contextlib import ExitStack

import numpy as np

import concourse.bass as bass
from concourse import mybir
from concourse.alu_op_type import AluOpType as ALU

F32 = mybir.dt.float32
F32R = mybir.dt.float32r
BF16 = mybir.dt.bfloat16
ACT = mybir.ActivationFunctionType
AX_X = mybir.AxisListType.X
AX_XY = mybir.AxisListType.XY

P = 128
BATCH = 8
TIME, FREQ = 750, 128
PATCH = 16
TOK = -(-TIME // PATCH) * (FREQ // PATCH)
TOKENS = BATCH * TOK
DIM = 256
HALVES = DIM // P
HEADS, HEAD = 16, 64
INNER = HEADS * HEAD
PAIRS = HEADS // 2
EXPERTS, FFN = 4, 1024
QFFN, QBLOCK = 768, 32
TILES = -(-TOK // P)
TILE_ROWS = [min(P, TOK - P * i) for i in range(TILES)]
BANK = 512
NEG = -1e30

VECTORS = ("L0_tok_b", "L0_tok_gamma", "L0_tok_beta", "L0_attn_bo", "L1_attn_phazor_real",
           "L1_attn_phazor_imag", "L1_attn_phazor_init_real", "L1_attn_phazor_init_imag",
           "L1_attn_last_conv_real", "L1_attn_last_conv_imag")
EPS_TOK, EPS_LN, PLUS_MAGIC, MINUS_MAGIC = range(4)


def scopes(nc):
    ctx = ExitStack()
    sb = lambda name, shape, dt=F32: ctx.enter_context(nc.sbuf_tensor(name, shape, dt))
    sem = lambda name: ctx.enter_context(nc.semaphore(name))
    return ctx, sb, sem


def clear(nc, sems):
    with nc.Block() as block:
        @block.gpsimd
        def _(pool):
            for s in sems:
                pool.sem_clear(s)


def paced(engine, step):
    for n in range(2):
        step(n, n, n)
    with engine.Fori(1, BATCH // 2 - 1) as i:
        for u in range(2):
            step(2 * i + u, u, 4)
    for n in range(BATCH - 2, BATCH):
        step(n, n % 2, n)


def tokens_of(n):
    return bass.ds(n * TOK, TOK)


STEPS_TO_NORM = 17


def recurrence_tables(block, sb, sem, vec, decay, tables, tables_dram):
    col = {n: sb(f"rec_{n}", [P, HALVES]) for n in
           ("square", "other", "size", "zero", "inv", "re", "im", "norm2", "root", "unit", "fix")}
    tmp = sb("rec_tmp", [P, 2, TOK])
    turn, feed = (tables[:, i, :, :, :] for i in range(2))
    step, decayed, rooted, tabled, stored = (sem(f"rec_{n}") for n in ("step", "decayed", "rooted", "tabled", "stored"))
    re, im = vec["L1_attn_phazor_real"], vec["L1_attn_phazor_imag"]
    pr, pi = vec["L1_attn_phazor_init_real"], vec["L1_attn_phazor_init_imag"]

    @block.scalar
    def _(act):
        act.wait_ge(step, 3)
        act.activation(decay[:], col["square"][:], ACT.Exp, scale=-1.0).then_inc(decayed, 1)
        act.wait_ge(step, STEPS_TO_NORM)
        act.activation(col["root"][:], col["norm2"][:], ACT.Sqrt).then_inc(rooted, 1)

    @block.sync
    def _(sp):
        sp.wait_ge(tabled, 1)
        sp.dma_start(tables_dram, tables[:]).then_inc(stored, 16)
        sp.wait_ge(stored, 16)

    @block.vector
    def _(dve):
        done = [0]

        def link(ins):
            done[0] += 1
            ins.then_inc(step, 1)
            dve.wait_ge(step, done[0])

        c = {n: t[:] for n, t in col.items()}
        tt = lambda o, x, y, op: link(dve.tensor_tensor(o, x, y, op))
        tt(c["square"], re, re, ALU.mult)
        tt(c["other"], im, im, ALU.mult)
        tt(c["square"], c["square"], c["other"], ALU.add)
        link(dve.tensor_scalar(c["size"], re, -1.0, None, ALU.mult))
        tt(c["size"], c["size"], re, ALU.max)
        tt(c["size"], c["size"], im, ALU.max)
        link(dve.tensor_scalar(c["other"], im, -1.0, None, ALU.mult))
        tt(c["size"], c["size"], c["other"], ALU.max)
        link(dve.tensor_scalar(c["zero"], c["size"], 0.0, None, ALU.is_equal))
        tt(c["size"], c["size"], c["zero"], ALU.add)
        link(dve.reciprocal(c["inv"], c["size"]))
        tt(c["re"], re, c["inv"], ALU.mult)
        tt(c["re"], c["re"], c["zero"], ALU.add)
        tt(c["im"], im, c["inv"], ALU.mult)
        tt(c["norm2"], c["re"], c["re"], ALU.mult)
        tt(c["other"], c["im"], c["im"], ALU.mult)
        tt(c["norm2"], c["norm2"], c["other"], ALU.add)
        assert done[0] == STEPS_TO_NORM
        dve.wait_ge(rooted, 1)
        link(dve.reciprocal(c["unit"], c["root"]))
        for _ in range(2):
            tt(c["fix"], c["unit"], c["unit"], ALU.mult)
            tt(c["fix"], c["fix"], c["norm2"], ALU.mult)
            link(dve.tensor_scalar(c["fix"], c["fix"], -0.5, 1.5, ALU.mult, ALU.add))
            tt(c["unit"], c["unit"], c["fix"], ALU.mult)
        for part, x in enumerate(("re", "im")):
            last = dve.tensor_tensor(turn[:, part, :, 0], c[x], c["unit"], ALU.mult)
        link(last)
        n = 1
        while n < TOK:
            k = min(n, TOK - n)
            for h in range(HALVES):
                for part in range(2):
                    last = dve.tensor_scalar(tmp[:, part, 0:k], turn[:, 1 - part, h, 0:k],
                                             turn[:, 1, h, n - 1:n], None, ALU.mult)
                link(last)
                for part, op in ((0, ALU.subtract), (1, ALU.add)):
                    last = dve.scalar_tensor_tensor(turn[:, part, h, n:n + k], turn[:, part, h, 0:k],
                                                    turn[:, 0, h, n - 1:n], tmp[:, part, 0:k], ALU.mult, op)
                link(last)
            n += k
        for h in range(HALVES):
            for part, x in enumerate((pi, pr)):
                last = dve.tensor_scalar(tmp[:, part, :], turn[:, 1, h, :], x[:, h:h + 1], None, ALU.mult)
            link(last)
            for part, (x, op) in enumerate(((pr, ALU.add), (pi, ALU.subtract))):
                last = dve.scalar_tensor_tensor(feed[:, part, h, :], turn[:, 0, h, :], x[:, h:h + 1],
                                                tmp[:, part, :], ALU.mult, op)
            link(last)
        dve.wait_ge(decayed, 1)
        dve.sem_inc(tabled, 1)


def tokenize(nc, psum, hid, patches_dram, w_dram, bias, loads, vec, decay, tables_dram):
    ctx, sb, sem = scopes(nc)
    with ctx:
        patch = sb("patch", [P, 2, TOKENS])
        w = sb("tok_w", [P, 2, DIM])
        parts = BATCH // 2
        loaded = [sem(f"tok_loaded{i}") for i in range(parts)]
        params, made, kept = sem("tok_params"), sem("tok_made"), sem("tok_kept")
        tables = sb("tables", [P, 2, 2, HALVES, TOK])
        with nc.Block() as block:
            @block.sync
            def _(sp):
                sp.dma_start(w[:], w_dram.rearrange("(c p) e -> p c e", p=P)).then_inc(params, 16)
                for i in range(parts):
                    cols = slice(2 * i * TOK, 2 * (i + 1) * TOK)
                    sp.dma_start(patch[:, :, cols], patches_dram[:, :, cols]).then_inc(loaded[i], 16)
                for to, source, loaded_too in loads:
                    sp.dma_start(to, source).then_inc(loaded_too, 16)

            recurrence_tables(block, sb, sem, vec, decay, tables, tables_dram)

            @block.tensor
            def _(pe):
                pe.wait_ge(params, 16)
                for i in range(parts):
                    pe.wait_ge(loaded[i], 16)
                    for u in range(2):
                        pe.wait_ge(kept, 2 * i + u + 1)
                        for m in range(HALVES):
                            for c in range(2):
                                last = pe.matmul(psum[:, 2 * u + m, 0:TOK], w[:, c, m * P:(m + 1) * P],
                                                 patch[:, c, tokens_of(2 * i + u)], start=(c == 0), stop=(c == 1))
                        last.then_inc(made, 1)

            @block.scalar
            def _(act):
                act.sem_inc(kept, 2)
                with act.Fori(0, BATCH // 2) as i:
                    for u in range(2):
                        act.wait_ge(made, 2 * i + u + 1)
                        for m in range(HALVES):
                            last = act.activation(hid[:, m, tokens_of(2 * i + u)], psum[:, 2 * u + m, 0:TOK],
                                                  ACT.Identity, bias=bias[:, m:m + 1])
                        last.then_inc(kept, 1)


def layernorm(nc, psum, sems, name, src, dst, consts, ones, eps, affine=None, load=None, ends=False, behind=None):
    ctx, sb, sem = scopes(nc)
    with ctx:
        square = sb(f"{name}_square", [P, 2, HALVES, TOK])
        std = sb(f"{name}_std", [P, 2, TOK])
        rstd = sb(f"{name}_rstd", [P, 2, TOK])
        mean_made, centered, squared, var_made, std_made, rstd_made, normed = sems
        clear(nc, sems)
        with nc.Block() as block:
            def batches(engine, step):
                for u in range(2):
                    step(u, u, False, True)
                with engine.Fori(1, BATCH // 2 - 1) as i:
                    for u in range(2):
                        step(2 * i + u, u, True, True)
                for u in range(2):
                    step(BATCH - 2 + u, u, True, False)

            @block.sync
            def _(sp):
                if load is not None:
                    sp.dma_start(load[0], load[1]).then_inc(load[2], 16)
                if load is not None and ends:
                    sp.wait_ge(load[2], 16)

            @block.tensor
            def _(pe):
                pe.sem_inc(var_made, 2)

                def mean(n, u):
                    pe.wait_ge(centered, n + 1)
                    for c in range(HALVES):
                        last = pe.matmul(psum[:, u, 0:TOK], ones[:], src[:, c, tokens_of(n)],
                                         start=(c == 0), stop=(c == HALVES - 1))
                    last.then_inc(mean_made, 1)

                def step(n, u, _, more):
                    if more:
                        mean(n + 2, u)
                    pe.wait_ge(std_made, n + 1)
                    pe.wait_ge(squared, n + 1)
                    for c in range(HALVES):
                        last = pe.matmul(psum[:, 2 + u, 0:TOK], ones[:], square[:, u, c, :],
                                         start=(c == 0), stop=(c == HALVES - 1))
                    last.then_inc(var_made, 1)

                mean(0, 0)
                mean(1, 1)
                batches(pe, step)

            @block.vector
            def _(dve):
                dve.sem_inc(centered, 2)
                dve.sem_inc(rstd_made, 2)

                def centre(n, u):
                    dve.wait_ge(mean_made, n + 1)
                    t = tokens_of(n)
                    dve.tensor_tensor(dst[:, :, t], src[:, :, t],
                                      psum[:, u:u + 1, 0:TOK].broadcast_to((P, HALVES, TOK)),
                                      ALU.subtract).then_inc(centered, 1)

                def step(n, u, _, more):
                    if more:
                        centre(n + 2, u)
                    dve.wait_ge(std_made, n + 3)
                    dve.wait_ge(normed, n + 1)
                    dve.reciprocal(rstd[:, u, :], std[:, u, :]).then_inc(rstd_made, 1)

                centre(0, 0)
                centre(1, 1)
                batches(dve, step)

            @block.gpsimd
            def _(pool):
                pool.sem_inc(normed, 2)

                def step(n, u, *_):
                    pool.wait_ge(rstd_made, n + 3)
                    t = tokens_of(n)
                    pool.tensor_tensor(dst[:, :, t], dst[:, :, t],
                                       rstd[:, u:u + 1, :].broadcast_to((P, HALVES, TOK)),
                                       ALU.mult).then_inc(normed, 1)

                batches(pool, step)

            @block.scalar
            def _(act):
                act.sem_inc(std_made, 2)

                def squares(n, u):
                    act.wait_ge(centered, n + 3)
                    act.wait_ge(var_made, n + 1)
                    act.activation(square[:, u, :, :], dst[:, :, tokens_of(n)], ACT.Square).then_inc(squared, 1)

                def scaled(n):
                    act.wait_ge(normed, n + 3)
                    for c in range(HALVES):
                        act.activation(dst[:, c, tokens_of(n)], dst[:, c, tokens_of(n)], ACT.Identity,
                                       scale=affine[0][:, c:c + 1], bias=affine[1][:, c:c + 1])

                def step(n, u, earlier, more):
                    act.wait_ge(var_made, n + 3)
                    act.wait_ge(rstd_made, n + 1)
                    act.activation(std[:, u, :], psum[:, 2 + u, 0:TOK], ACT.Sqrt,
                                   bias=consts[:, eps:eps + 1]).then_inc(std_made, 1)
                    if more:
                        squares(n + 2, u)
                    if earlier and affine is not None:
                        scaled(n - 2)

                squares(0, 0)
                squares(1, 1)
                batches(act, step)
                if affine is not None:
                    scaled(BATCH - 2)
                    scaled(BATCH - 1)

            if behind is not None:
                behind(block)


def split_weights(block, jobs, arrived, high_made, low_made):
    @block.scalar
    def _(act):
        for i, (stage, high, _) in enumerate(jobs):
            act.wait_ge(arrived[i], 16)
            act.activation(high, stage, ACT.Copy).then_inc(high_made, 1)

    @block.vector
    def _(dve):
        for i, (stage, high, low) in enumerate(jobs):
            cols = slice(0, stage.shape[1] * 3 // 4)
            dve.wait_ge(high_made, i + 1)
            dve.tensor_tensor(low[:, cols], stage[:, cols], high[:, cols].bitcast(F32),
                              ALU.subtract).then_inc(low_made, 1)

    @block.gpsimd
    def _(pool):
        for i, (stage, high, low) in enumerate(jobs):
            cols = slice(stage.shape[1] * 3 // 4, stage.shape[1])
            pool.wait_ge(high_made, i + 1)
            pool.tensor_tensor(low[:, cols], stage[:, cols], high[:, cols].bitcast(F32),
                               ALU.subtract).then_inc(low_made, 1)


def attention(nc, psum, norm, hid_dram, weights, a, ident, bo):
    ctx, sb, sem = scopes(nc)
    with ctx:
        wq, wk, wv = ([w.rearrange("p (c n) -> p c n", c=2) for w in weights[n]] for n in range(3))
        wo = [w.rearrange("p (c n) -> p c n", c=PAIRS) for w in weights[3]]
        x = [sb(f"x_{part}", [P, 2, TOK], F32R) for part in ("high", "low")]
        v = [sb(f"v_{part}", [P, TILES, INNER], F32R) for part in ("high", "low")]
        qk = [sb(f"qk_{part}", [P, 2, 2, TOK], F32R) for part in ("high", "low")]
        raw = sb("raw", [P, 2, TOK])
        swapped = sb("swapped", [P, 2, TOK])
        cosined = sb("cosined", [P, 2, TOK])
        rotated = sb("rotated", [P, 2, TOK])
        cos = sb("rope_cos", [P, 2, TOK])
        sin = sb("rope_sin", [P, 2, TOK])
        neg_max = sb("neg_max", [P, 2, 4])
        row_sum = sb("row_sum", [P, 2, 4])
        inv_sum = sb("inv_sum", [P, 2, 4])
        probs = sb("probs", [P, 2, TILES, TOK])
        diag = sb("diag", [P, 2, TILES, P])
        pt = [sb(f"pt_{part}", [P, 2, 2, TOK], F32R) for part in ("high", "low")]
        o = [sb(f"o_{part}", [P, PAIRS, TOK], F32R) for part in ("high", "low")]
        resid = sb("resid", [P, HALVES, TOK])
        mask = sb("mask", [P, P], BF16)
        ident_b = sb("ident_b", [P, P], BF16)
        mask_f = sb("mask_f", [P, P])
        holder = sb("holder", [P, 2 * PAIRS])
        (tables_in, masks_made, resid_in, cleared, x_high, x_low, v_made, v_high, v_low, proj_made,
         raw_made, swap_made, rope_made, rot_made, qk_high, qk_ready, scores_made, max_made, exp_made,
         inv_made, diag_made, turned, pt_high, pt_ready, mixed, o_high, o_ready, out_made, out_kept) = (
            sem(n) for n in
            "tables_in masks_made resid_in cleared x_high x_low v_made v_high v_low proj_made "
            "raw_made swap_made rope_made rot_made qk_high qk_ready scores_made max_made exp_made "
            "inv_made diag_made turned pt_high pt_ready mixed o_high o_ready out_made out_kept".split())
        CR_RAW, CR_ROT, CR_SCORES, CR_EXP, CR_TURN, CR_PT, CR_MIX, CR_O, CR_OUT = 1, 2, 4, 2, 2, 1, 2, 1, 1
        BANK_PROJ, BANK_O, BANK_PT, OUT_BANKS = 7, 6, 4, (6, 2)
        three = ((0, 0), (0, 1), (1, 0))
        swap = [i ^ 1 for i in range(32)]

        def score_bank(par, it):
            if it == 2:
                return psum[0:TILE_ROWS[2], 2 * par + 1, 0:TOK]
            return psum[:, 2 * par, P * it:P * it + P * (it + 1)]

        def probs_t(j):
            return (0, 0, TOK) if j == 0 else (1, 0, TOK - P) if j == 1 else (1, TOK - P, TOK - 2 * P)

        with nc.Block() as block:
            @block.sync
            def _(sp):
                sp.dma_start(cos[:], a["c_cos"]).then_inc(tables_in, 16)
                sp.dma_start(sin[:], a["c_sin"]).then_inc(tables_in, 16)
                sp.dma_start(mask_f[:], a["c_mask"]).then_inc(tables_in, 16)
                with sp.Fori(0, BATCH) as b:
                    sp.wait_ge(out_kept, 2 * b + CR_OUT)
                    sp.dma_start(resid[:], hid_dram[:, :, tokens_of(b)]).then_inc(resid_in, 16)

            AHEAD, LEAD = 6, 5

            @block.tensor
            def _(pe):
                pe.sem_inc(scores_made, CR_SCORES)
                pe.sem_inc(turned, CR_TURN)
                pe.sem_inc(mixed, CR_MIX)
                pe.wait_ge(cleared, 3)

                def project(b, n):
                    c, k = n // 2, n % 2
                    if n == 0:
                        pe.wait_ge(x_low, b + 1)
                    pe.wait_ge(raw_made, 16 * b + n + CR_RAW)
                    w = (wq, wk)[k]
                    for i, (hw, hx) in enumerate(three):
                        for half in range(2):
                            last = pe.matmul(psum[:, BANK_PROJ, 0:TOK], w[hw][:, half, P * c:P * (c + 1)],
                                             x[hx][:, half, :], start=(i == half == 0), stop=(i == 2 and half == 1))
                    last.then_inc(proj_made, 1)

                def scores(b, h):
                    c, par = h // 2, h % 2
                    r = slice(HEAD * par, HEAD * (par + 1))
                    pe.wait_ge(qk_ready, 16 * b + 2 * c + 2)
                    pe.wait_ge(exp_made, 16 * b + h + 1)
                    for it in range(TILES):
                        ni, dst = TILE_ROWS[it], score_bank(par, it)
                        nj = P * it + ni
                        for i, (hq, hk) in enumerate(three):
                            pe.matmul(dst, qk[hq][r, c % 2, 0, P * it:P * it + ni], qk[hk][r, c % 2, 1, 0:nj],
                                      start=(i == 0), stop=False)
                        last = pe.matmul(dst[:, P * it:nj], ident_b[:, 0:ni], mask[:, 0:ni],
                                         start=False, stop=True)
                    last.then_inc(scores_made, 1)

                def turn(b, h):
                    pe.wait_ge(diag_made, 16 * b + h + 1)
                    pe.wait_ge(pt_ready, 16 * b + h + CR_PT)
                    for j in range(TILES):
                        bank, col, _ = probs_t(j)
                        for it in range(j, TILES):
                            ni, nj = TILE_ROWS[it], TILE_ROWS[j]
                            at = col + P * (it - j)
                            last = pe.matmul(psum[0:nj, BANK_PT + bank, at:at + ni],
                                             probs[0:ni, h % 2, it, P * j:P * j + nj],
                                             diag[0:ni, h % 2, it, 0:ni], start=True, stop=True)
                    last.then_inc(turned, 1)

                def mix(b, h):
                    c = h // 2
                    pe.wait_ge(pt_ready, 16 * b + h + 1 + CR_PT)
                    pe.wait_ge(o_ready, 16 * b + h + CR_O)
                    for j in range(TILES):
                        bank, col, n = probs_t(j)
                        for i, (hv, hp) in enumerate(three):
                            nj = TILE_ROWS[j]
                            last = pe.matmul(psum[:, BANK_O, P * j:TOK], v[hv][0:nj, j, P * c:P * (c + 1)],
                                             pt[hp][0:nj, h % 2, bank, col:col + n],
                                             start=(i == j == 0), stop=(i == 2 and j == TILES - 1))
                    last.then_inc(mixed, 1)

                def values(tiles):
                    for t in tiles:
                        for half in range(2):
                            for i, (hw, hx) in enumerate(three):
                                for c in range(2):
                                    last = pe.matmul(psum[0:TILE_ROWS[t], 2 * t + half, :],
                                                     x[hx][:, c, P * t:P * t + TILE_ROWS[t]],
                                                     wv[hw][:, c, BANK * half:BANK * (half + 1)],
                                                     start=(i == c == 0), stop=(i == 2 and c == 1))
                            last.then_inc(v_made, 1)

                def output(b, m):
                    if m == 0:
                        pe.wait_ge(o_ready, 16 * b + HEADS + CR_O)
                    else:
                        pe.wait_ge(v_low, 6 * b + 6 + 3)
                    for i, (hw, ho) in enumerate(three):
                        for c in range(PAIRS):
                            last = pe.matmul(psum[:, OUT_BANKS[m], 0:TOK], wo[hw][:, c, P * m:P * (m + 1)],
                                             o[ho][:, c, :], start=(i == c == 0), stop=(i == 2 and c == PAIRS - 1))
                    last.then_inc(out_made, 1)

                def begin(b, before=None):
                    pe.wait_ge(exp_made, 16 * b + CR_EXP)
                    values((0, 1))
                    if before is not None:
                        mix(before, HEADS - 1)
                    pe.wait_ge(pt_ready, 16 * b + CR_PT)
                    values((2,))
                    if before is not None:
                        output(before, 0)
                        output(before, 1)
                    pe.wait_ge(v_low, 6 * b + 4)
                    scores(b, 0)
                    project(b, LEAD)
                    if before is not None:
                        pe.wait_ge(out_kept, 2 * b + CR_OUT)
                    pe.wait_ge(v_low, 6 * b + 6)
                    scores(b, 1)

                def heads(b, more=True):
                    for h in range(HEADS):
                        turn(b, h)
                        if h + 2 < HEADS:
                            scores(b, h + 2)
                        if h:
                            mix(b, h - 1)
                        if h + AHEAD < HEADS:
                            project(b, h + AHEAD)
                        elif h >= HEADS - LEAD and more:
                            project(b + 1, h - HEADS + LEAD)

                for n in range(LEAD):
                    project(0, n)
                pe.wait_ge(masks_made, 2)
                begin(0)
                with pe.Fori(0, BATCH - 1) as b:
                    heads(b)
                    begin(b + 1, b)
                heads(BATCH - 1, False)
                mix(BATCH - 1, HEADS - 1)
                output(BATCH - 1, 0)
                for i, (hw, ho) in enumerate(three):
                    for c in range(PAIRS):
                        last = pe.matmul(psum[:, OUT_BANKS[1], 0:TOK], wo[hw][:, c, P:2 * P],
                                         o[ho][:, c, :], start=(i == c == 0), stop=(i == 2 and c == PAIRS - 1))
                last.then_inc(out_made, 1)

            @block.scalar
            def _(act):
                act.sem_inc(exp_made, CR_EXP)
                act.sem_inc(raw_made, CR_RAW)

                def x_split(b):
                    act.activation(x[0][:], norm[:, :, tokens_of(b)], ACT.Copy).then_inc(x_high, 1)

                def raw_copy(b, n):
                    act.wait_ge(proj_made, 16 * b + n + 1)
                    act.wait_ge(rot_made, 16 * b + n + 1)
                    act.activation(raw[:, n % 2, :], psum[:, BANK_PROJ, 0:TOK], ACT.Copy).then_inc(raw_made, 1)

                def qk_split(b, n):
                    c = n // 2
                    act.wait_ge(rot_made, 16 * b + n + 1 + CR_ROT)
                    act.wait_ge(scores_made, 16 * b + 2 * c + CR_SCORES - 2)
                    act.activation(qk[0][:, c % 2, n % 2, :], rotated[:, n % 2, :], ACT.Copy).then_inc(qk_high, 1)

                def exps(b, h):
                    act.wait_ge(max_made, 16 * b + h + 1)
                    act.wait_ge(turned, 16 * b + h + 1)
                    for it in range(TILES):
                        ni = TILE_ROWS[it]
                        last = act.activation(probs[0:ni, h % 2, it, 0:P * it + ni], score_bank(h % 2, it),
                                              ACT.Exp, bias=neg_max[0:ni, h % 2, it:it + 1],
                                              accum_out=row_sum[0:ni, h % 2, it:it + 1])
                    last.then_inc(exp_made, 1)

                def turned_high(b, h):
                    act.wait_ge(turned, 16 * b + h + 1 + CR_TURN)
                    act.wait_ge(mixed, 16 * b + h + 1)
                    act.activation(pt[0][:, h % 2, :, :], psum[:, BANK_PT:BANK_PT + 2, 0:TOK],
                                   ACT.Copy).then_inc(pt_high, 1)

                def out_high(b, h):
                    r = slice(HEAD * (h % 2), HEAD * (h % 2 + 1))
                    act.wait_ge(mixed, 16 * b + h + 1 + CR_MIX)
                    act.activation(o[0][r, h // 2, :], psum[r, BANK_O, 0:TOK], ACT.Copy).then_inc(o_high, 1)

                def lead(b, h):
                    n = h - HEADS + LEAD
                    if n >= 0:
                        raw_copy(b, n)
                    if n >= 2:
                        qk_split(b, n - 2)

                def begin(b, before=None):
                    if before is not None:
                        out_high(before, HEADS - 1)
                    for t in range(TILES):
                        for half in range(2):
                            act.wait_ge(v_made, 6 * b + 2 * t + half + 1)
                            act.wait_ge(mixed, 16 * b + CR_MIX)
                            act.activation(v[0][0:TILE_ROWS[t], t, BANK * half:BANK * (half + 1)],
                                           psum[0:TILE_ROWS[t], 2 * t + half, :], ACT.Copy).then_inc(v_high, 1)
                    qk_split(b, LEAD - 2)
                    exps(b, 0)
                    raw_copy(b, LEAD)

                def heads(b, more):
                    for h in range(HEADS):
                        if h + 1 < HEADS:
                            exps(b, h + 1)
                        turned_high(b, h)
                        if h:
                            out_high(b, h - 1)
                        if h + AHEAD - 2 < HEADS:
                            qk_split(b, h + AHEAD - 2)
                        if h + AHEAD < HEADS:
                            raw_copy(b, h + AHEAD)
                        if h == HEADS - AHEAD - 1 and more:
                            x_split(b + 1)
                        if more:
                            lead(b + 1, h)

                act.wait_ge(cleared, 3)
                x_split(0)
                for h in range(HEADS):
                    lead(0, h)
                begin(0)
                with act.Fori(0, BATCH - 1) as b:
                    heads(b, True)
                    begin(b + 1, b)
                heads(BATCH - 1, False)
                out_high(BATCH - 1, HEADS - 1)

            @block.gpsimd
            def _(pool):
                pool.sem_inc(rot_made, CR_ROT)

                def qk_split(b, n):
                    c, k = n // 2, n % 2
                    pool.wait_ge(qk_high, 16 * b + n + 1)
                    pool.tensor_tensor(qk[1][:, c % 2, k, :], rotated[:, k, :],
                                       qk[0][:, c % 2, k, :].bitcast(F32), ALU.subtract).then_inc(qk_ready, 1)

                pool.wait_ge(tables_in, 48)
                with pool.Fori(0, BATCH) as b:
                    for n in range(2 * PAIRS):
                        k = n % 2
                        pool.wait_ge(raw_made, 16 * b + n + 1 + CR_RAW)
                        pool.tensor_tensor(cosined[:, k, :], raw[:, k, :], cos[:, k, :],
                                           ALU.mult).then_inc(rope_made, 1)
                        pool.wait_ge(swap_made, 16 * b + n + 1)
                        pool.tensor_tensor(swapped[:, k, :], swapped[:, k, :], sin[:, k, :],
                                           ALU.mult).then_inc(rope_made, 1)
                        pool.wait_ge(rope_made, 32 * b + 2 * n + 2)
                        pool.tensor_tensor(rotated[:, k, :], cosined[:, k, :], swapped[:, k, :],
                                           ALU.add).then_inc(rot_made, 1)
                        if n:
                            qk_split(b, n - 1)
                    qk_split(b, 2 * PAIRS - 1)

            @block.vector
            def _(dve):
                dve.sem_inc(pt_ready, CR_PT)
                dve.sem_inc(o_ready, CR_O)
                dve.sem_inc(out_kept, CR_OUT)
                dve.memset(row_sum[:], 1.0).then_inc(cleared, 1)
                dve.memset(psum[:, BANK_PT:BANK_PT + 2, 0:TOK], 0.0).then_inc(cleared, 1)
                dve.memset(neg_max[:], 0.0).then_inc(cleared, 1)
                dve.wait_ge(cleared, 3)

                def x_split(b):
                    dve.wait_ge(x_high, b + 1)
                    dve.tensor_tensor(x[1][:], norm[:, :, tokens_of(b)], x[0][:].bitcast(F32),
                                      ALU.subtract).then_inc(x_low, 1)

                def swap_pairs(b, n):
                    dve.wait_ge(raw_made, 16 * b + n + 1 + CR_RAW)
                    dve.memset(holder[:, n:n + 1], 0.0)
                    dve.stream_shuffle(swapped[:, n % 2, :], raw[:, n % 2, :], swap).then_inc(swap_made, 1)

                def maxima(b, h):
                    dve.wait_ge(scores_made, 16 * b + h + 1 + CR_SCORES)
                    for it in range(TILES):
                        ni = TILE_ROWS[it]
                        last = dve.tensor_reduce(neg_max[0:ni, h % 2, it:it + 1], score_bank(h % 2, it),
                                                 AX_X, ALU.max, negate=True)
                    last.then_inc(max_made, 1)

                def diagonals(b, h):
                    dve.wait_ge(exp_made, 16 * b + h + 1 + CR_EXP)
                    dve.reciprocal(inv_sum[:, h % 2, 0:TILES], row_sum[:, h % 2, 0:TILES]).then_inc(inv_made, 1)
                    dve.wait_ge(inv_made, 16 * b + h + 1)
                    dve.tensor_tensor(diag[:, h % 2, :, :],
                                      ident[:].rearrange("p (o n) -> p o n", o=1).broadcast_to((P, TILES, P)),
                                      inv_sum[:, h % 2, 0:TILES].rearrange("p (t o) -> p t o", o=1)
                                      .broadcast_to((P, TILES, P)), ALU.mult).then_inc(diag_made, 1)

                def turned_low(b, h):
                    dve.wait_ge(pt_high, 16 * b + h + 1)
                    dve.tensor_tensor(pt[1][:, h % 2, :, :], psum[:, BANK_PT:BANK_PT + 2, 0:TOK],
                                      pt[0][:, h % 2, :, :].bitcast(F32), ALU.subtract).then_inc(pt_ready, 1)

                def out_low(b, h):
                    r = slice(HEAD * (h % 2), HEAD * (h % 2 + 1))
                    dve.wait_ge(o_high, 16 * b + h + 1)
                    dve.tensor_tensor(o[1][r, h // 2, :], psum[r, BANK_O, 0:TOK],
                                      o[0][r, h // 2, :].bitcast(F32), ALU.subtract).then_inc(o_ready, 1)

                def residual(b, m):
                    dve.wait_ge(out_made, 2 * b + m + 1)
                    dve.wait_ge(resid_in, 16 * b + 16)
                    dve.scalar_tensor_tensor(norm[:, m, tokens_of(b)], psum[:, OUT_BANKS[m], 0:TOK],
                                             bo[:, m:m + 1], resid[:, m, :], ALU.add, ALU.add).then_inc(out_kept, 1)

                def begin(b, before=None):
                    if before is not None:
                        out_low(before, HEADS - 1)
                    for t in range(TILES):
                        for half in range(2):
                            dve.wait_ge(v_high, 6 * b + 2 * t + half + 1)
                            cols = slice(BANK * half, BANK * (half + 1))
                            dve.tensor_tensor(v[1][0:TILE_ROWS[t], t, cols],
                                              psum[0:TILE_ROWS[t], 2 * t + half, :],
                                              v[0][0:TILE_ROWS[t], t, cols].bitcast(F32),
                                              ALU.subtract).then_inc(v_low, 1)
                    if before is not None:
                        residual(before, 0)
                        residual(before, 1)
                    maxima(b, 0)
                    diagonals(b, 0)
                    swap_pairs(b, LEAD)
                    maxima(b, 1)

                def heads(b, more):
                    for h in range(HEADS):
                        if h + 1 < HEADS:
                            diagonals(b, h + 1)
                        turned_low(b, h)
                        if h + 2 < HEADS:
                            maxima(b, h + 2)
                        if h:
                            out_low(b, h - 1)
                        if h + AHEAD < HEADS:
                            swap_pairs(b, h + AHEAD)
                        if h == HEADS - AHEAD - 1 and more:
                            x_split(b + 1)
                        if h >= HEADS - LEAD and more:
                            swap_pairs(b + 1, h - HEADS + LEAD)

                x_split(0)
                dve.wait_ge(tables_in, 48)
                dve.tensor_copy(mask[:], mask_f[:]).then_inc(masks_made, 1)
                dve.tensor_copy(ident_b[:], ident[:]).then_inc(masks_made, 1)
                for n in range(LEAD):
                    swap_pairs(0, n)
                begin(0)
                with dve.Fori(0, BATCH - 1) as b:
                    heads(b, True)
                    begin(b + 1, b)
                heads(BATCH - 1, False)
                out_low(BATCH - 1, HEADS - 1)
                for m in range(HALVES):
                    residual(BATCH - 1, m)


EXPERT_COLS = 2 * 2 * FFN + FFN // P * DIM
SLICE = EXPERT_COLS // BATCH


def route(nc, psum, norm, gates_t, x, first, w, bias, params, staged, staged_in, ident):
    ctx, sb, sem = scopes(nc)
    with ctx:
        tiles = BATCH * TILES
        odds = sb("odds", [P, tiles, EXPERTS])
        top = sb("odds_top", [P, tiles])
        beats = sb("beats", [P, tiles, EXPERTS])
        rank = sb("rank", [P, tiles, EXPERTS])
        total = sb("odds_total", [P, tiles])
        cleared, logits_made, shifted, exp_made, step, gates_made, turned, kept = (
            sem(f"route_{n}") for n in ("cleared", "logits_made", "shifted", "exp_made", "step",
                                        "gates_made", "turned", "kept"))
        x_high, x_low, w_high, w_low = (sem(f"route_{n}") for n in ("x_high", "x_low", "w_high", "w_low"))
        logits = psum[:, 0, 0:tiles * EXPERTS].rearrange("p (t e) -> p t e", e=EXPERTS)
        wide = lambda x: x[:].rearrange("p (t o) -> p t o", o=1).broadcast_to((P, tiles, EXPERTS))
        with nc.Block() as block:
            @block.gpsimd
            def _(pool):
                with pool.Fori(0, BATCH) as b:
                    pool.wait_ge(w_high, b + 1)
                    cols = bass.ds(b * SLICE, SLICE)
                    pool.tensor_tensor(first[1][:, cols], staged[:, cols], first[0][:, cols].bitcast(F32),
                                       ALU.subtract).then_inc(w_low, 1)

            @block.tensor
            def _(pe):
                pe.wait_ge(params, 48)
                pe.wait_ge(cleared, 1)
                for t in range(tiles):
                    n, at = TILE_ROWS[t % TILES], TOK * (t // TILES) + P * (t % TILES)
                    for c in range(2):
                        last = pe.matmul(logits[0:n, t, :], norm[:, c, at:at + n], w[:, c, :],
                                         start=(c == 0), stop=(c == 1))
                last.then_inc(logits_made, 1)
                pe.wait_ge(gates_made, 1)
                for t in range(tiles):
                    n = TILE_ROWS[t % TILES]
                    last = pe.transpose(psum[0:EXPERTS, t // TILES, P * (t % TILES):P * (t % TILES) + n],
                                        odds[0:n, t, :], ident[0:n, 0:n])
                    if t % TILES == TILES - 1:
                        last.then_inc(turned, 1)

            @block.scalar
            def _(act):
                with act.Fori(0, BATCH) as b:
                    act.activation(x[0][:, :, tokens_of(b)], norm[:, :, tokens_of(b)], ACT.Copy).then_inc(x_high, 1)
                act.wait_ge(staged_in, 16)
                with act.Fori(0, BATCH) as b:
                    cols = bass.ds(b * SLICE, SLICE)
                    act.activation(first[0][:, cols], staged[:, cols], ACT.Copy).then_inc(w_high, 1)
                act.wait_ge(shifted, 1)
                act.activation(odds[:], odds[:], ACT.Exp).then_inc(exp_made, 1)
                for b in range(BATCH):
                    act.wait_ge(turned, b + 1)
                    act.activation(gates_t[:, tokens_of(b)], psum[0:EXPERTS, b, 0:TOK], ACT.Copy).then_inc(kept, 1)

            @block.vector
            def _(dve):
                done = [0]

                def link(ins):
                    done[0] += 1
                    ins.then_inc(step, 1)
                    dve.wait_ge(step, done[0])

                dve.memset(psum[:, 0, 0:tiles * EXPERTS], 0.0).then_inc(cleared, 1)
                for e in range(EXPERTS):
                    last = dve.memset(rank[:, :, e:e + 1], float(EXPERTS - 1 - e))
                link(last)
                with dve.Fori(0, BATCH) as b:
                    dve.wait_ge(x_high, b + 1)
                    dve.tensor_tensor(x[1][:, :, tokens_of(b)], norm[:, :, tokens_of(b)],
                                      x[0][:, :, tokens_of(b)].bitcast(F32), ALU.subtract).then_inc(x_low, 1)
                dve.wait_ge(params, 48)
                dve.wait_ge(logits_made, 1)
                link(dve.tensor_tensor(odds[:], logits, bias[:].rearrange("p (o e) -> p o e", o=1)
                                       .broadcast_to((P, tiles, EXPERTS)), ALU.add))
                link(dve.tensor_reduce(top[:], odds[:], AX_X, ALU.max))
                dve.tensor_tensor(odds[:], odds[:], wide(top), ALU.subtract).then_inc(shifted, 1)
                dve.wait_ge(exp_made, 1)
                for d in range(1, EXPERTS):
                    k = EXPERTS - d
                    link(dve.tensor_tensor(beats[:, :, 0:k], odds[:, :, 0:k], odds[:, :, d:], ALU.is_ge))
                    link(dve.tensor_tensor(rank[:, :, 0:k], rank[:, :, 0:k], beats[:, :, 0:k], ALU.subtract))
                    link(dve.tensor_tensor(rank[:, :, d:], rank[:, :, d:], beats[:, :, 0:k], ALU.add))
                link(dve.tensor_scalar(rank[:], rank[:], 1.5, None, ALU.is_lt))
                link(dve.tensor_tensor(odds[:], odds[:], rank[:], ALU.mult))
                link(dve.tensor_reduce(total[:], odds[:], AX_X, ALU.add))
                link(dve.reciprocal(total[:], total[:]))
                dve.tensor_tensor(odds[:], odds[:], wide(total), ALU.mult).then_inc(gates_made, 1)


def experts(nc, psum, hid, x, gates_t, select, first, even, a, ln_sems, consts, ones, vec, decay, tables_dram):
    ctx, sb, sem = scopes(nc)
    with ctx:
        chunks = FFN // P
        weights = [first, [sb(f"expert_w1_{part}", [P, EXPERT_COLS], F32R) for part in ("high", "low")]]
        stage = sb("expert_stage", [P, SLICE])
        silu = sb("silu", [P, 2, TOK])
        act_f = sb("expert_act", [P, 2, TOK])
        act_hl = [sb(f"expert_act_{part}", [P, 2, TOK], F32R) for part in ("high", "low")]
        gate = sb("gate", [P, 1, TOK])
        gated_out = sb("gated_out", [P, HALVES, TOK])
        three = ((0, 0), (0, 1), (1, 0))
        BANK_OUT, BANK_STAT, BANK_GATE = 4, 6, 7
        mean_made, centered, squared, var_made, std_made, rstd_made, normed = ln_sems
        tables_in, fed_made, scanned, im_made, re_made, re_added, joined = (
            sem(f"rec_{n}") for n in ("tables_in", "fed_made", "scanned", "im_made", "re_made", "re_added", "joined"))
        last_parts = (vec["L1_attn_last_conv_real"], vec["L1_attn_last_conv_imag"])

        GATE_AT, FETCH_AT, ADD_AT, MEAN_AT, VAR_AT = 3, 2, 1, 2, 4

        def expert(e, block, turn=None, feed=None, state=None, fed=None, norm=None, square=None, std=None, rstd=None):
            now, coming = weights[e % 2], weights[(e + 1) % 2]
            fetch = e + 1 < EXPERTS
            done = BATCH * e
            recur = not fetch

            def batches(engine, batch):
                for b in range(4):
                    batch(b, b % 2, b)
                with engine.Fori(2, BATCH // 2) as i:
                    for u in range(2):
                        batch(2 * i + u, u, BATCH)

            @block.sync
            def _(sp):
                if recur:
                    sp.wait_ge(down_made, chunks * done + 2)
                    sp.dma_start(turn[:], tables_dram[:, 0, :, :, :]).then_inc(tables_in, 16)
                    sp.dma_start(feed[:], tables_dram[:, 1, :, :, :]).then_inc(tables_in, 16)
                if fetch:
                    with sp.Fori(0, BATCH) as b:
                        sp.wait_ge(w_low, done + b + 1)
                        sp.dma_start(stage[:], a["experts"][e + 1, :, bass.ds(b * SLICE, SLICE)]).then_inc(w_in, 16)

            def split_high(act, b):
                act.wait_ge(w_in, 16 * (done + b) + 16)
                act.activation(coming[0][:, bass.ds(b * SLICE, SLICE)], stage[:], ACT.Copy).then_inc(w_high, 1)

            @block.tensor
            def _(pe):
                if e == 0:
                    pe.sem_inc(down_made, 2)
                    pe.sem_inc(gate_made, 1)
                if recur:
                    pe.sem_inc(var_made, 1)

                def up(b, f, ends=False):
                    pe.wait_ge(act_made, chunks * (done + b) + f + 1)
                    t, w = tokens_of(b + f // chunks), now
                    if ends and f >= chunks:
                        t, w = tokens_of(0), coming
                    for k in range(2):
                        for i, (hw, hx) in enumerate(three):
                            for c in range(2):
                                at = (2 * k + c) * FFN + P * (f % chunks)
                                last = pe.matmul(psum[:, 2 * k + f % 2, 0:TOK], w[hw][:, at:at + P],
                                                 x[hx][:, c, t], start=(i == c == 0), stop=(i == 2 and c == 1))
                    last.then_inc(up_made, 1)

                def down(b, f):
                    if f == 0:
                        pe.wait_ge(out_read, done + b + 1)
                    pe.wait_ge(low_made, chunks * (done + b) + f + 1 + 2)
                    for m in range(HALVES):
                        for i, (hw, hx) in enumerate(three):
                            at = 4 * FFN + DIM * f + P * m
                            last = pe.matmul(psum[:, BANK_OUT + m, 0:TOK], now[hw][:, at:at + P],
                                             act_hl[hx][:, f % 2, :], start=(i == f == 0),
                                             stop=(i == 2 and f == chunks - 1))
                    last.then_inc(down_made, 1)

                def mean(n):
                    pe.wait_ge(added, done + n + 2)
                    pe.wait_ge(std_made, n + 1)
                    for c in range(HALVES):
                        last = pe.matmul(psum[:, BANK_STAT, 0:TOK], ones[:], hid[:, c, tokens_of(n)],
                                         start=(c == 0), stop=(c == HALVES - 1))
                    last.then_inc(mean_made, 1)

                def variance(n):
                    pe.wait_ge(squared, n + 1)
                    for c in range(HALVES):
                        last = pe.matmul(psum[:, BANK_STAT, 0:TOK], ones[:], square[:, c, :],
                                         start=(c == 0), stop=(c == HALVES - 1))
                    last.then_inc(var_made, 1)

                def batch(b, before=True, ends=False):
                    for f in range(chunks):
                        if ends and fetch and f + 2 == chunks:
                            pe.wait_ge(w_low, done + BATCH + 1)
                        if fetch or not ends or f + 2 < chunks:
                            up(b, f + 2, ends)
                        if recur and before and f == MEAN_AT:
                            mean(b - 1)
                        if recur and before and f == VAR_AT:
                            variance(b - 1)
                        if f == GATE_AT:
                            pe.wait_ge(gate_kept, done + b + 1)
                            pe.matmul(psum[:, BANK_GATE, 0:TOK], select[:, P * e:P * (e + 1)],
                                      gates_t[:, tokens_of(b)], start=True, stop=True).then_inc(gate_made, 1)
                        down(b, f)

                if e == 0:
                    up(0, 0)
                    up(0, 1)
                batch(0, False)
                batch(1)
                with pe.Fori(1, BATCH // 2 - 1) as i:
                    for u in range(2):
                        batch(2 * i + u)
                batch(BATCH - 2)
                batch(BATCH - 1, ends=True)
                if recur:
                    mean(BATCH - 1)
                    variance(BATCH - 1)

            @block.scalar
            def _(act):
                if e == 0:
                    act.sem_inc(gate_kept, 1)
                if recur:
                    act.sem_inc(std_made, 1)

                def squares(n, u):
                    act.wait_ge(centered, n + 1)
                    act.wait_ge(var_made, n + 1)
                    act.activation(square[:], norm[:, u, :, :], ACT.Square).then_inc(squared, 1)

                def deviation(n):
                    act.wait_ge(var_made, n + 1 + 1)
                    act.wait_ge(rstd_made, n + 1)
                    act.activation(std[:], psum[:, BANK_STAT, 0:TOK], ACT.Sqrt,
                                   bias=consts[:, EPS_LN:EPS_LN + 1]).then_inc(std_made, 1)

                def batch(b, u, known):
                    for f in range(chunks):
                        act.wait_ge(up_made, chunks * (done + b) + f + 1)
                        act.activation(silu[:, f % 2, :], psum[:, f % 2, 0:TOK], ACT.Silu).then_inc(silu_made, 1)
                        act.wait_ge(act_made, chunks * (done + b) + f + 1 + 2)
                        act.wait_ge(down_made, chunks * (done + b) + f + 1)
                        act.activation(act_hl[0][:, f % 2, :], act_f[:, f % 2, :], ACT.Copy).then_inc(high_made, 1)
                        if f == GATE_AT + 1:
                            act.wait_ge(gate_made, done + b + 2)
                            act.wait_ge(out_read, done + b + 1)
                            act.activation(gate[:, 0, :], psum[:, BANK_GATE, 0:TOK],
                                           ACT.Copy).then_inc(gate_kept, 1)
                        if f == FETCH_AT and fetch:
                            split_high(act, b)
                        if recur and known >= 1 and f == VAR_AT:
                            squares(b - 1, 1 - u)
                        if recur and known >= 1 and f == VAR_AT + 2:
                            deviation(b - 1)

                batches(act, batch)
                if recur:
                    squares(BATCH - 1, 1)
                    deviation(BATCH - 1)

            @block.vector
            def _(dve):
                if e == 0:
                    dve.sem_inc(act_made, 2)
                    dve.sem_inc(out_read, 1)
                if recur:
                    dve.sem_inc(rstd_made, 1)
                    dve.sem_inc(scanned, 2)
                    dve.sem_inc(joined, 1)

                def gated(n):
                    dve.wait_ge(gate_kept, done + n + 2)
                    dve.wait_ge(added, done + n + 1)
                    dve.wait_ge(down_made, chunks * (done + n) + chunks + 2)
                    dve.tensor_tensor(gated_out[:], psum[:, BANK_OUT:BANK_OUT + 2, 0:TOK],
                                      gate[:].broadcast_to((P, HALVES, TOK)), ALU.mult).then_inc(out_read, 1)

                def centre(n, u):
                    dve.wait_ge(mean_made, n + 1)
                    dve.wait_ge(fed_made, 2 * n + 2)
                    dve.tensor_tensor(norm[:, u, :, :], hid[:, :, tokens_of(n)],
                                      psum[:, BANK_STAT:BANK_STAT + 1, 0:TOK].broadcast_to((P, HALVES, TOK)),
                                      ALU.subtract).then_inc(centered, 1)

                def inverse(n):
                    dve.wait_ge(std_made, n + 1 + 1)
                    dve.reciprocal(rstd[:], std[:]).then_inc(rstd_made, 1)

                def normalise(n, u):
                    dve.wait_ge(rstd_made, n + 1 + 1)
                    dve.tensor_tensor(norm[:, u, :, :], norm[:, u, :, :],
                                      rstd[:].rearrange("p (o t) -> p o t", o=1).broadcast_to((P, HALVES, TOK)),
                                      ALU.mult).then_inc(normed, 1)

                def scan(n, k):
                    dve.wait_ge(fed_made, 2 * n + k + 1 + 4)
                    dve.wait_ge(joined, n + 1)
                    for h in range(HALVES):
                        last = dve.tensor_tensor_scan(state[:, k, h, :], decay[:, h:h + 1].broadcast_to((P, TOK)),
                                                      fed[:, k, h, :], last_parts[k][:, h:h + 1],
                                                      ALU.mult, ALU.add)
                    last.then_inc(scanned, 1)

                def real_part(n):
                    dve.wait_ge(scanned, 2 * n + 1 + 2)
                    dve.tensor_tensor(state[:, 0, :, :], state[:, 0, :, :], turn[:, 0, :, :],
                                      ALU.mult).then_inc(re_made, 1)

                def add_real(n):
                    dve.wait_ge(re_made, n + 1)
                    t = tokens_of(n)
                    dve.tensor_tensor(hid[:, :, t], hid[:, :, t], state[:, 0, :, :], ALU.add).then_inc(re_added, 1)

                def subtract_imaginary(n):
                    dve.wait_ge(re_added, n + 1)
                    dve.wait_ge(im_made, n + 1)
                    t = tokens_of(n)
                    dve.tensor_tensor(hid[:, :, t], hid[:, :, t], state[:, 1, :, :],
                                      ALU.subtract).then_inc(joined, 1)

                def recurrence(b, u, known, f):
                    first, second, third = (known >= k and known - k < BATCH for k in (1, 2, 3))
                    if first and f == 4:
                        centre(b - 1, 1 - u)
                    if first and f == 7:
                        inverse(b - 1)
                    if second and f == 0:
                        normalise(b - 2, u)
                    if second and f in (5, 6):
                        scan(b - 2, f - 5)
                    if third and f == 2:
                        real_part(b - 3)
                    if third and f == 3:
                        add_real(b - 3)
                    if third and f == 4:
                        subtract_imaginary(b - 3)

                def batch(b, u, known):
                    for f in range(chunks):
                        if f == 1 and (known >= 1 or e > 0):
                            gated(b - 1)
                        dve.wait_ge(silu_made, chunks * (done + b) + f + 1)
                        dve.wait_ge(low_made, chunks * (done + b) + f + 1)
                        dve.tensor_tensor(act_f[:, f % 2, :], psum[:, 2 + f % 2, 0:TOK], silu[:, f % 2, :],
                                          ALU.mult).then_inc(act_made, 1)
                        if recur:
                            recurrence(b, u, min(known, BATCH - 1), f)

                batches(dve, batch)
                if recur:
                    gated(BATCH - 1)
                    for b in range(BATCH, BATCH + 3):
                        for f in range(chunks):
                            recurrence(b, b % 2, b, f)

            @block.gpsimd
            def _(pool):
                if e == 0:
                    pool.sem_inc(w_low, 1)
                    pool.sem_inc(low_made, 2)
                    pool.sem_inc(added, 1)
                if recur:
                    pool.sem_inc(fed_made, 4)
                    pool.wait_ge(tables_in, 32)

                def feeding(n, u, k):
                    pool.wait_ge(normed, n + 1)
                    pool.wait_ge(scanned, 2 * n + k + 1)
                    pool.tensor_tensor(fed[:, k, :, :], norm[:, u, :, :], feed[:, k, :, :],
                                       ALU.mult).then_inc(fed_made, 1)

                def imaginary_part(n):
                    pool.wait_ge(scanned, 2 * n + 2 + 2)
                    pool.tensor_tensor(state[:, 1, :, :], state[:, 1, :, :], turn[:, 1, :, :],
                                       ALU.mult).then_inc(im_made, 1)

                def recurrence(b, u, known, f):
                    second = known >= 2 and known - 2 < BATCH
                    if second and f in (2, 4):
                        feeding(b - 2, u, f // 2 - 1)
                    if second and f == 7:
                        imaginary_part(b - 2)

                def split_low(b):
                    pool.wait_ge(w_high, done + b + 1)
                    cols = bass.ds(b * SLICE, SLICE)
                    pool.tensor_tensor(coming[1][:, cols], stage[:], coming[0][:, cols].bitcast(F32),
                                       ALU.subtract).then_inc(w_low, 1)

                def add(n):
                    pool.wait_ge(out_read, done + n + 2)
                    t = tokens_of(BATCH - 1 if isinstance(n, int) and n < 0 else n)
                    pool.tensor_tensor(hid[:, :, t], hid[:, :, t], gated_out[:], ALU.add).then_inc(added, 1)

                def batch(b, u, known):
                    for f in range(chunks):
                        pool.wait_ge(high_made, chunks * (done + b) + f + 1)
                        pool.tensor_tensor(act_hl[1][:, f % 2, :], act_f[:, f % 2, :],
                                           act_hl[0][:, f % 2, :].bitcast(F32), ALU.subtract).then_inc(low_made, 1)
                        if f == ADD_AT and (known >= 1 or e > 0):
                            add(b - 1)
                        if f == FETCH_AT and fetch:
                            split_low(b)
                        if recur:
                            recurrence(b, u, min(known, BATCH - 1), f)

                batches(pool, batch)
                if recur:
                    add(BATCH - 1)
                    for b in range(BATCH, BATCH + 2):
                        for f in range(chunks):
                            recurrence(b, b % 2, b, f)

        sems = [sem(f"expert_{n}") for n in
                ("w_in", "w_high", "w_low", "up_made", "silu_made", "act_made", "high_made",
                 "low_made", "down_made", "gate_made", "gate_kept", "out_read", "added")]
        (w_in, w_high, w_low, up_made, silu_made, act_made, high_made, low_made, down_made,
         gate_made, gate_kept, out_read, added) = sems
        clear(nc, ln_sems)
        with nc.Block() as block:
            for e in range(EXPERTS - 1):
                expert(e, block)
            even.close()
            buffers = {n: ctx.enter_context(nc.sbuf_tensor(f"recur_{n}", [P, *shape, TOK], F32, side="right"))
                       for n, shape in (("turn", (2, HALVES)), ("feed", (2, HALVES)), ("state", (2, HALVES)),
                                        ("fed", (2, HALVES)), ("norm", (2, HALVES)), ("square", (HALVES,)),
                                        ("std", ()), ("rstd", ()))}
            expert(EXPERTS - 1, block, **buffers)


MAGIC = 1.5 * 2.0 ** 23
ACT_MAX = 32767.0
WEIGHT_MAX = 7.0
SIG_STEPS = 65536.0
TINY = 1e-12
QCHUNKS = QFFN // P
QCOLS = QFFN * DIM // P
RMAX = bass.bass_isa.ReduceOp.max


def quantised_weights(block, sb, sem, psum, a, ident, up_gate, down, std_made):
    w = sb("q_raw", [P, 3 * QCOLS])
    scale = sb("q_scale", [P, 3 * QCOLS // QBLOCK])
    inv = sb("q_inv", [P, 3 * QCOLS // QBLOCK])
    w_in = [sem(f"q_w_in{m}") for m in range(3)]
    step, rounded, made, turned, high_made, low_made = (
        sem(f"q_{n}") for n in ("step", "rounded", "made", "turned", "high_made", "low_made"))
    blocks = w[:].rearrange("p (n k) -> p n k", k=QBLOCK)
    NB = QCOLS // QBLOCK
    per_block = lambda x, some: x[:, some].rearrange("p (n o) -> p n o", o=1).broadcast_to((P, NB, QBLOCK))
    groups = []
    for m in range(2):
        for c in range(HALVES):
            for g in range(0, QCHUNKS, 3):
                groups.append((m * QCOLS + g * DIM + c * P, DIM,
                               [up_gate[k][:, c, m * QFFN + g * P:m * QFFN + (g + 3) * P] for k in range(2)]))
    for m in range(HALVES):
        for g in range(0, QCHUNKS, 3):
            groups.append((2 * QCOLS + m * QFFN + g * P, P,
                           [down[k][:, g:g + 3, m * P:(m + 1) * P] for k in range(2)]))

    def group_bank(n, like):
        x = psum[:, n % 8, 0:3 * P]
        return x if len(like.shape) == 2 else x.rearrange("p (k n) -> p k n", k=3)

    @block.sync
    def _(sp):
        for i, name in enumerate(("L1_ffn_w_up", "L1_ffn_w_gate")):
            sp.dma_start(w[:, i * QCOLS:(i + 1) * QCOLS].rearrange("p (t n) -> p t n", n=DIM),
                         a[name].rearrange("(t p) n -> p t n", p=P)).then_inc(w_in[i], 16)
        sp.dma_start(w[:, 2 * QCOLS:].rearrange("p (t n) -> p t n", n=QFFN),
                     a["L1_ffn_w_down"].rearrange("(t p) n -> p t n", p=P)).then_inc(w_in[2], 16)

    @block.vector
    def _(dve):
        done = [0]

        def link(ins):
            done[0] += 1
            ins.then_inc(step, 1)
            dve.wait_ge(step, done[0])

        for m in range(3):
            own, some = slice(m * QCOLS, (m + 1) * QCOLS), slice(m * NB, (m + 1) * NB)
            dve.wait_ge(w_in[m], 16)
            link(dve.tensor_reduce(scale[:, some], blocks[:, some, :], AX_X, ALU.max,
                                   apply_absolute_value=True))
            link(dve.tensor_scalar(scale[:, some], scale[:, some], 1.0 / WEIGHT_MAX, TINY,
                                   ALU.mult, ALU.max))
            link(dve.reciprocal(inv[:, some], scale[:, some]))
            link(dve.tensor_tensor(blocks[:, some, :], blocks[:, some, :], per_block(inv, some), ALU.mult))
            dve.tensor_scalar(w[:, own], w[:, own], MAGIC, MAGIC, ALU.add, ALU.subtract).then_inc(rounded, 1)
        for n, (_, _, dst) in enumerate(groups):
            dve.wait_ge(high_made, n + 1)
            dve.tensor_tensor(dst[1], group_bank(n, dst[1]), dst[0].bitcast(F32),
                              ALU.subtract).then_inc(low_made, 1)

    @block.gpsimd
    def _(pool):
        for m in range(3):
            some = slice(m * NB, (m + 1) * NB)
            pool.wait_ge(rounded, m + 1)
            pool.tensor_tensor(blocks[:, some, :], blocks[:, some, :], per_block(scale, some),
                               ALU.mult).then_inc(made, 1)

    @block.tensor
    def _(pe):
        pe.wait_ge(std_made, BATCH + 2)
        for n, (at, apart, _) in enumerate(groups):
            pe.wait_ge(made, n // 4 + 1)
            if n >= 8:
                pe.wait_ge(low_made, n - 7)
            for k in range(3):
                last = pe.transpose(psum[:, n % 8, P * k:P * (k + 1)],
                                    w[:, at + apart * k:at + apart * k + P], ident[:])
            last.then_inc(turned, 1)

    @block.scalar
    def _(act):
        for n, (_, _, dst) in enumerate(groups):
            act.wait_ge(turned, n + 1)
            act.activation(dst[0], group_bank(n, dst[0]), ACT.Copy).then_inc(high_made, 1)


def absolute_max(nc, peaks, x):
    with nc.Block() as block:
        @block.vector
        def _(dve):
            with dve.Fori(0, BATCH) as b:
                dve.tensor_reduce(peaks[:, bass.ds(b, 1)], x[:, :, tokens_of(b)], AX_XY, ALU.max, apply_absolute_value=True)


def step_size(nc, name, peaks, scale, inv, times=None):
    ctx, sb, sem = scopes(nc)
    with ctx:
        own = sb(f"{name}_own", [P, 1])
        peak = sb(f"{name}_peak", [P, 1])
        owned, shared, step = sem(f"{name}_owned"), sem(f"{name}_shared"), sem(f"{name}_step")
        with nc.Block() as block:
            @block.gpsimd
            def _(pool):
                pool.wait_ge(owned, 1)
                pool.partition_all_reduce(peak[:], own[:], P, RMAX).then_inc(shared, 1)

            @block.vector
            def _(dve):
                dve.tensor_reduce(own[:], peaks[:], AX_X, ALU.max).then_inc(owned, 1)
                dve.wait_ge(shared, 1)
                n = 0
                if times is not None:
                    dve.tensor_tensor(peak[:], peak[:], times, ALU.mult).then_inc(step, 1)
                    n = 1
                    dve.wait_ge(step, n)
                dve.tensor_scalar(scale, peak[:], 1.0 / ACT_MAX, TINY, ALU.mult, ALU.max).then_inc(step, 1)
                dve.wait_ge(step, n + 1)
                dve.reciprocal(inv, scale).then_inc(step, 1)
                if times is not None:
                    dve.wait_ge(step, n + 2)
                    dve.tensor_tensor(inv, inv, times, ALU.mult)


def quantised_ffn(nc, psum, ln_sems, hid, a, consts, ones, ident, up_gate, down, out):
    ctx, sb, sem = scopes(nc)
    up_dram = nc.dram_tensor("up_spill", [P, QCHUNKS, TOKENS], F32, kind="Internal").ap()
    three = ((0, 0), (0, 1), (1, 0))
    with ctx:
        gate = sb("q_gate", [P, QCHUNKS, TOKENS])
        peaks = sb("q_peaks", [P, 4, BATCH])
        steps = sb("q_steps", [P, 12])
        (S_X, I_X, S_UP, I_UP, S_GATE, I_GATE, S_ACT, I_ACT, S_BOTH, S_OUT, I_OUT) = (
            steps[:, i:i + 1] for i in range(11))
        magic, minus_magic = consts[:, PLUS_MAGIC:PLUS_MAGIC + 1], consts[:, MINUS_MAGIC:MINUS_MAGIC + 1]
        X_, UP_, GATE_, OUT_ = range(4)
        two = BATCH // 2

        with ExitStack() as part:
            norm = part.enter_context(nc.sbuf_tensor("norm4", [P, HALVES, TOKENS], F32))
            with ExitStack() as behind:
                behind_sb = lambda name, shape: behind.enter_context(nc.sbuf_tensor(name, shape, F32, side="right"))
                behind_sem = lambda name: behind.enter_context(nc.semaphore(name))
                layernorm(nc, psum, ln_sems, "ln_q", hid, norm, consts, ones, EPS_LN,
                          behind=lambda block: quantised_weights(block, behind_sb, behind_sem, psum, a, ident,
                                                                 up_gate, down, ln_sems[4]))
            absolute_max(nc, peaks[:, X_, :], norm)
            step_size(nc, "q_x", peaks[:, X_, :], S_X, I_X)
            q = part.enter_context(nc.sbuf_tensor("q_tokens", [P, 2, HALVES, TOK], F32))
            qhl = [part.enter_context(nc.sbuf_tensor(f"q_tokens_{k}", [P, 2, HALVES, TOK], F32R)) for k in ("high", "low")]
            up = part.enter_context(nc.sbuf_tensor("q_up", [P, QCHUNKS, TOK], F32))
            q_made, high_made, low_made, made, kept, up_out, peak_made = (
                part.enter_context(nc.semaphore(f"q1_{n}")) for n in
                ("q_made", "high_made", "low_made", "made", "kept", "up_out", "peak_made"))
            block = part.enter_context(nc.Block())
            BANKS = 6

            @block.vector
            def _(dve):
                dve.sem_inc(peak_made, 2)

                def rounded(n, u):
                    dve.tensor_scalar(q[:, u, :, :], norm[:, :, tokens_of(n)], I_X, MAGIC,
                                      ALU.mult, ALU.add).then_inc(q_made, 1)
                    dve.wait_ge(high_made, n + 1)
                    dve.scalar_tensor_tensor(qhl[1][:, u, :, :], q[:, u, :, :], MAGIC,
                                             qhl[0][:, u, :, :].bitcast(F32), ALU.subtract,
                                             ALU.subtract).then_inc(low_made, 1)

                def batch(n, u, more=True):
                    dve.wait_ge(kept, 12 * n + 6 + BANKS)
                    dve.tensor_reduce(peaks[:, UP_, bass.ds(n, 1)], up[:], AX_XY, ALU.max,
                                      apply_absolute_value=True).then_inc(peak_made, 1)
                    if more:
                        rounded(n + 1, 1 - u)
                    dve.wait_ge(kept, 12 * n + 12 + BANKS)
                    dve.tensor_reduce(peaks[:, GATE_, bass.ds(n, 1)], gate[:, :, tokens_of(n)], AX_XY, ALU.max,
                                      apply_absolute_value=True)

                rounded(0, 0)
                with dve.Fori(0, two - 1) as i:
                    for u in range(2):
                        batch(2 * i + u, u)
                batch(BATCH - 2, 0)
                batch(BATCH - 1, 1, False)

            @block.scalar
            def _(act):
                act.sem_inc(kept, BANKS)
                act.sem_inc(up_out, 16)

                def high(n, u):
                    act.wait_ge(q_made, n + 1)
                    act.activation(qhl[0][:, u, :, :], q[:, u, :, :], ACT.Identity,
                                   bias=minus_magic).then_inc(high_made, 1)

                def batch(n, u, more=True):
                    for j in range(2 * QCHUNKS):
                        act.wait_ge(made, 12 * n + j + 1)
                        if j == 0:
                            act.wait_ge(up_out, 16 * n + 16)
                            act.wait_ge(peak_made, n + 2)
                        dst = up[:, j, :] if j < QCHUNKS else gate[:, j - QCHUNKS, tokens_of(n)]
                        act.activation(dst, psum[:, j % BANKS, 0:TOK], ACT.Copy, scale=S_X).then_inc(kept, 1)
                        if j == 2 * QCHUNKS - 3 and more:
                            high(n + 1, 1 - u)

                high(0, 0)
                with act.Fori(0, two - 1) as i:
                    for u in range(2):
                        batch(2 * i + u, u)
                batch(BATCH - 2, 0)
                batch(BATCH - 1, 1, False)

            @block.tensor
            def _(pe):
                with pe.Fori(0, two) as i:
                    for u in range(2):
                        n = 2 * i + u
                        pe.wait_ge(low_made, n + 1)
                        for j in range(2 * QCHUNKS):
                            pe.wait_ge(kept, 12 * n + j + 1)
                            for k, (hw, hx) in enumerate(three):
                                for c in range(HALVES):
                                    last = pe.matmul(psum[:, j % BANKS, 0:TOK], up_gate[hw][:, c, P * j:P * (j + 1)],
                                                     qhl[hx][:, u, c, :], start=(k == c == 0), stop=(k == 2 and c == 1))
                            last.then_inc(made, 1)

            @block.sync
            def _(sp):
                with sp.Fori(0, BATCH) as n:
                    sp.wait_ge(kept, 12 * n + 6 + BANKS)
                    sp.dma_start(up_dram[:, :, tokens_of(n)], up[:]).then_inc(up_out, 16)
                sp.wait_ge(up_out, 16 * BATCH + 16)

        step_size(nc, "q_up", peaks[:, UP_, :], S_UP, I_UP)
        step_size(nc, "q_gate", peaks[:, GATE_, :], S_GATE, I_GATE)

        UP_BUFFERS = 4
        middle = ctx.enter_context(ExitStack())
        up = middle.enter_context(nc.sbuf_tensor("q_up2", [P, UP_BUFFERS, QCHUNKS, TOK], F32))
        up_in = [sem(f"q3_up_in{u}") for u in range(UP_BUFFERS)]

        with ExitStack() as part:
            sig = part.enter_context(nc.sbuf_tensor("q_sig", [P, 2, QCHUNKS, TOK], F32))
            scaled, rounded, sig_made, sig_scaled, sig_ready, prod_made = (
                part.enter_context(nc.semaphore(f"q2_{n}")) for n in
                ("scaled", "rounded", "sig_made", "sig_scaled", "sig_ready", "prod_made"))
            block = part.enter_context(nc.Block())

            @block.vector
            def _(dve):
                def front(n):
                    g = gate[:, :, tokens_of(n)]
                    dve.tensor_scalar(g, g, I_GATE, MAGIC, ALU.mult, ALU.add).then_inc(scaled, 1)
                    dve.wait_ge(scaled, n + 1)
                    dve.tensor_scalar(g, g, MAGIC, S_GATE, ALU.subtract, ALU.mult).then_inc(rounded, 1)

                def back(n, u):
                    dve.wait_ge(sig_scaled, n + 1)
                    dve.tensor_scalar(sig[:, u, :, :], sig[:, u, :, :], MAGIC + SIG_STEPS - 1, MAGIC,
                                      ALU.min, ALU.subtract).then_inc(sig_ready, 1)

                def peak(n):
                    dve.wait_ge(prod_made, n + 1 + 2)
                    dve.tensor_reduce(peaks[:, X_, bass.ds(n, 1)], gate[:, :, tokens_of(n)], AX_XY, ALU.max,
                                      apply_absolute_value=True)

                def step(n, u, known):
                    if known + 1 < BATCH:
                        front(n + 1)
                    back(n, u)
                    if known:
                        peak(n - 1)

                front(0)
                paced(dve, step)
                peak(BATCH - 1)

            @block.sync
            def _(sp):
                for n in range(UP_BUFFERS):
                    sp.dma_start(up[:, n, :, :], up_dram[:, :, tokens_of(n)]).then_inc(up_in[n], 16)

            @block.scalar
            def _(act):
                with act.Fori(0, two) as i:
                    for u in range(2):
                        n = 2 * i + u
                        act.wait_ge(rounded, n + 1)
                        act.wait_ge(prod_made, n + 1)
                        act.activation(sig[:, u, :, :], gate[:, :, tokens_of(n)], ACT.Sigmoid).then_inc(sig_made, 1)
                        act.wait_ge(sig_made, n + 1)
                        act.activation(sig[:, u, :, :], sig[:, u, :, :], ACT.Identity, scale=SIG_STEPS,
                                       bias=magic).then_inc(sig_scaled, 1)

            @block.gpsimd
            def _(pool):
                pool.sem_inc(prod_made, 2)
                with pool.Fori(0, two) as i:
                    for u in range(2):
                        n = 2 * i + u
                        pool.wait_ge(sig_ready, n + 1)
                        g = gate[:, :, tokens_of(n)]
                        pool.tensor_tensor(g, g, sig[:, u, :, :], ALU.mult).then_inc(prod_made, 1)

        step_size(nc, "q_act", peaks[:, X_, :], S_ACT, I_ACT)

        with ExitStack() as part:
            act_scaled, up_scaled, up_scaled_too, up_rounded, prod_made = (
                part.enter_context(nc.semaphore(f"q3_{n}")) for n in
                ("act_scaled", "up_scaled", "up_scaled_too", "up_rounded", "prod_made"))
            own, pools = slice(0, 1), slice(1, QCHUNKS)
            block = part.enter_context(nc.Block())
            buffer = lambda n: up[:, n % UP_BUFFERS, :, :]

            @block.sync
            def _(sp):
                for n in range(UP_BUFFERS, BATCH):
                    sp.wait_ge(prod_made, n - UP_BUFFERS + 1)
                    sp.dma_start(buffer(n), up_dram[:, :, tokens_of(n)]).then_inc(up_in[n % UP_BUFFERS], 16)

            @block.scalar
            def _(act):
                for n in range(BATCH):
                    g = gate[:, :, tokens_of(n)]
                    act.activation(g, g, ACT.Identity, scale=I_ACT, bias=magic).then_inc(act_scaled, 1)
                    act.wait_ge(up_scaled, n + 1)
                    act.wait_ge(up_scaled_too, n + 1)
                    act.activation(buffer(n), buffer(n), ACT.Identity, bias=minus_magic).then_inc(up_rounded, 1)

            @block.gpsimd
            def _(pool):
                for n in range(BATCH):
                    pool.wait_ge(up_in[n % UP_BUFFERS], 16 * (n // UP_BUFFERS) + 16)
                    pool.tensor_scalar(buffer(n)[:, pools, :], buffer(n)[:, pools, :], I_UP, MAGIC,
                                       ALU.mult, ALU.add).then_inc(up_scaled_too, 1)

            @block.vector
            def _(dve):
                dve.tensor_scalar(S_BOTH, S_ACT, S_UP, 1.0 / SIG_STEPS, ALU.mult, ALU.mult)

                def scale_up(n):
                    dve.wait_ge(up_in[n % UP_BUFFERS], 16 * (n // UP_BUFFERS) + 16)
                    dve.tensor_scalar(buffer(n)[:, own, :], buffer(n)[:, own, :], I_UP, MAGIC,
                                      ALU.mult, ALU.add).then_inc(up_scaled, 1)

                def peak(n):
                    dve.wait_ge(prod_made, n + 1)
                    dve.tensor_reduce(peaks[:, OUT_, n:n + 1], gate[:, :, tokens_of(n)], AX_XY, ALU.max,
                                      apply_absolute_value=True)

                scale_up(0)
                for n in range(BATCH):
                    if n + 1 < BATCH:
                        scale_up(n + 1)
                    if n:
                        peak(n - 1)
                    dve.wait_ge(act_scaled, n + 1)
                    dve.wait_ge(up_rounded, n + 1)
                    g = gate[:, :, tokens_of(n)]
                    dve.scalar_tensor_tensor(g, g, MAGIC, buffer(n), ALU.subtract, ALU.mult).then_inc(prod_made, 1)
                peak(BATCH - 1)

        step_size(nc, "q_out", peaks[:, OUT_, :], S_OUT, I_OUT, times=S_BOTH)

        middle.close()

        with ExitStack() as part:
            q = part.enter_context(nc.sbuf_tensor("q_prod", [P, 2, QCHUNKS, TOK], F32))
            qhl = [part.enter_context(nc.sbuf_tensor(f"q_prod_{k}", [P, 2, QCHUNKS, TOK], F32R)) for k in ("high", "low")]
            result = part.enter_context(nc.sbuf_tensor("result", [P, 2, HALVES, TOK], F32))
            stored = [part.enter_context(nc.semaphore(f"q4_stored{u}")) for u in range(2)]
            q_made, high_made, low_made, made, result_made = (
                part.enter_context(nc.semaphore(f"q4_{n}")) for n in
                ("q_made", "high_made", "low_made", "made", "result_made"))
            block = part.enter_context(nc.Block())

            @block.vector
            def _(dve):
                dve.sem_inc(low_made, 2)
                dve.sem_inc(result_made, 2)

                def rounded(n, u):
                    dve.wait_ge(low_made, n + 1)
                    dve.tensor_scalar(q[:, u, :, :], gate[:, :, tokens_of(n)], I_OUT, MAGIC,
                                      ALU.mult, ALU.add).then_inc(q_made, 1)

                def low(n, u):
                    dve.wait_ge(high_made, n + 1)
                    dve.wait_ge(made, n + 1)
                    dve.scalar_tensor_tensor(qhl[1][:, u, :, :], q[:, u, :, :], MAGIC,
                                             qhl[0][:, u, :, :].bitcast(F32),
                                             ALU.subtract, ALU.subtract).then_inc(low_made, 1)

                def step(n, u, known):
                    if known + 2 < BATCH:
                        rounded(n + 2, u)
                    if known + 1 < BATCH:
                        low(n + 1, 1 - u)
                    dve.wait_ge(made, n + 1 + 2)
                    if u == 0:
                        dve.wait_ge(stored[0], 8 * n + 16)
                    else:
                        dve.wait_ge(stored[1], 8 * n + 8)
                    dve.scalar_tensor_tensor(result[:, u, :, :], psum[:, 2 * u:2 * u + 2, 0:TOK], S_OUT,
                                             hid[:, :, tokens_of(n)], ALU.mult, ALU.add).then_inc(result_made, 1)

                rounded(0, 0)
                rounded(1, 1)
                low(0, 0)
                paced(dve, step)

            @block.scalar
            def _(act):
                with act.Fori(0, two) as i:
                    for u in range(2):
                        n = 2 * i + u
                        act.wait_ge(q_made, n + 1)
                        act.wait_ge(made, n + 1)
                        act.activation(qhl[0][:, u, :, :], q[:, u, :, :], ACT.Identity, bias=minus_magic).then_inc(high_made, 1)

            @block.tensor
            def _(pe):
                pe.sem_inc(made, 2)
                with pe.Fori(0, two) as i:
                    for u in range(2):
                        n = 2 * i + u
                        pe.wait_ge(low_made, n + 1 + 2)
                        pe.wait_ge(result_made, n + 1)
                        for m in range(HALVES):
                            for k, (hw, hx) in enumerate(three):
                                for c in range(QCHUNKS):
                                    last = pe.matmul(psum[:, 2 * u + m, 0:TOK], down[hw][:, c, P * m:P * (m + 1)],
                                                     qhl[hx][:, u, c, :], start=(k == c == 0),
                                                     stop=(k == 2 and c == QCHUNKS - 1))
                        last.then_inc(made, 1)

            @block.sync
            def _(sp):
                for u in range(2):
                    sp.sem_inc(stored[u], 16)
                with sp.Fori(0, two) as i:
                    for u in range(2):
                        n = 2 * i + u
                        sp.wait_ge(result_made, n + 1 + 2)
                        sp.dma_start(out[:, :, tokens_of(n)], result[:, u, :, :]).then_inc(stored[u], 16)
                for u in range(2):
                    sp.wait_ge(stored[u], 16 * two + 16)


def audio_tower(nc, a, out):
    with ExitStack() as ctx:
        psum = ctx.enter_context(nc.psum_tensor("psum", [P, 8, BANK], F32))
        hid_dram = nc.dram_tensor("hid_spill", [P, HALVES, TOKENS], F32, kind="Internal").ap()
        norm = ctx.enter_context(nc.sbuf_tensor("norm", [P, HALVES, TOKENS], F32))
        consts = ctx.enter_context(nc.sbuf_tensor("consts", [P, 4], F32))
        ones = ctx.enter_context(nc.sbuf_tensor("ones", [P, P], F32))
        decay = ctx.enter_context(nc.sbuf_tensor("decay", [P, HALVES], F32))
        tables_dram = nc.dram_tensor("tables_spill", [P, 2, 2, HALVES, TOK], F32, kind="Internal").ap()
        ident = ctx.enter_context(nc.sbuf_tensor("ident", [P, P], F32))
        vectors = ctx.enter_context(nc.sbuf_tensor("vectors", [P, len(VECTORS), HALVES], F32))
        vec = {name: vectors[:, i, :] for i, name in enumerate(VECTORS)}
        ln_sems = [ctx.enter_context(nc.semaphore(f"ln_{n}")) for n in
                   ("mean_made", "centered", "squared", "var_made", "std_made", "rstd_made", "normed")]
        const_in = ctx.enter_context(nc.semaphore("const_in"))
        with nc.Block() as block:
            @block.sync
            def _(sp):
                sp.dma_start(consts[:], a["c_columns"]).then_inc(const_in, 16)
                sp.dma_start(ident[:], a["c_ident"]).then_inc(const_in, 16)
                sp.dma_start(vectors[:], a["vectors"]).then_inc(const_in, 16)
                sp.wait_ge(const_in, 48)

            @block.vector
            def _(dve):
                dve.memset(ones[:], 1.0 / DIM)

        with ExitStack() as attn:
            matrices = ("L0_attn_Wq", "L0_attn_Wk", "L0_attn_Wv", "L0_attn_Wo")
            cols = DIM * INNER // P
            weights = [[attn.enter_context(nc.sbuf_tensor(f"{n}_{part}", [P, cols], F32R))[:]
                        for part in ("high", "low")] for n in matrices]
            with ExitStack() as early:
                arrived = [early.enter_context(nc.semaphore(f"{n}_arrived")) for n in matrices]
                spilled = early.enter_context(nc.semaphore("hid_spilled"))
                split_sems = [early.enter_context(nc.semaphore(f"attn_w_{part}_made")) for part in ("high", "low")]
                staged = [early.enter_context(nc.sbuf_tensor(f"{n}_staged", [P, cols], F32))[:] for n in matrices]
                with nc.sbuf_tensor("hid", [P, HALVES, TOKENS], F32) as hid:
                    loads = [(stage.rearrange("p (c n) -> p c n", n=a[n].shape[1]),
                              a[n].rearrange("(c p) n -> p c n", p=P), sem)
                             for stage, n, sem in zip(staged, matrices, arrived)]
                    tokenize(nc, psum, hid, a["patches"], a["L0_tok_W"], vec["L0_tok_b"], loads,
                             vec, decay, tables_dram)
                    layernorm(nc, psum, ln_sems, "ln_tok", hid, hid, consts, ones, EPS_TOK,
                              (vec["L0_tok_gamma"], vec["L0_tok_beta"]))
                    layernorm(nc, psum, ln_sems, "ln_attn", hid, norm, consts, ones, EPS_LN,
                              load=(hid_dram, hid[:], spilled), ends=True,
                              behind=lambda block: split_weights(
                                  block, [(staged[i], *weights[i]) for i in range(4)], arrived, *split_sems))
            attention(nc, psum, norm, hid_dram, weights, a, ident, vec["L0_attn_bo"])
        with ExitStack() as moe:
            gates_t = moe.enter_context(nc.sbuf_tensor("gates_t", [EXPERTS, TOKENS], F32))
            x = [moe.enter_context(nc.sbuf_tensor(f"xm_{part}", [P, HALVES, TOKENS], F32R)) for part in ("high", "low")]
            select = moe.enter_context(nc.sbuf_tensor("expert_select", [EXPERTS, EXPERTS * P], F32))
            even = moe.enter_context(ExitStack())
            first = [even.enter_context(nc.sbuf_tensor(f"expert_w0_{part}", [P, EXPERT_COLS], F32R, side="right"))
                     for part in ("high", "low")]
            with nc.sbuf_tensor("norm2", [P, HALVES, TOKENS], F32) as norm2, \
                    nc.sbuf_tensor("first_staged", [P, EXPERT_COLS], F32) as staged, \
                    nc.sbuf_tensor("router_w", [P, 2, EXPERTS], F32) as router_w, \
                    nc.sbuf_tensor("router_bias", [P, EXPERTS], F32) as bias, \
                    nc.semaphore("first_staged_in") as staged_in, nc.semaphore("router_params") as params:

                def small_loads(block):
                    @block.sync
                    def _(sp):
                        sp.dma_start(router_w[:], a["L0_ffn_router_w"].rearrange("(c p) e -> p c e", p=P)) \
                            .then_inc(params, 16)
                        sp.dma_start(bias[:], a["router_b"]).then_inc(params, 16)
                        sp.dma_start(select[:], a["c_select"]).then_inc(params, 16)

                layernorm(nc, psum, ln_sems, "ln_ffn", norm, norm2, consts, ones, EPS_LN,
                          load=(staged[:], a["experts"][0], staged_in), behind=small_loads)
                route(nc, psum, norm2, gates_t, x, first, router_w, bias, params, staged, staged_in, ident)
            experts(nc, psum, norm, x, gates_t, select, first, even, a, ln_sems, consts, ones, vec, decay, tables_dram)
        hid = norm
        up_gate = [ctx.enter_context(nc.sbuf_tensor(f"up_gate_{part}", [P, HALVES, 2 * QFFN], F32R))
                   for part in ("high", "low")]
        down = [ctx.enter_context(nc.sbuf_tensor(f"down_{part}", [P, QCHUNKS, DIM], F32R))
                for part in ("high", "low")]
        quantised_ffn(nc, psum, ln_sems, hid, a, consts, ones, ident, up_gate, down, out)


def constants():
    columns = np.zeros((P, 4), np.float32)
    columns[:, EPS_TOK] = 1e-6
    columns[:, EPS_LN] = 1e-5
    columns[:, PLUS_MAGIC] = MAGIC
    columns[:, MINUS_MAGIC] = -MAGIC
    inv_freq = np.float32(1.0) / np.float32(10000.0) ** (np.arange(0, HEAD, 2, dtype=np.float32) / np.float32(HEAD))
    angle = np.arange(TOK, dtype=np.float32)[:, None] * inv_freq[None, :]
    pair = (np.arange(P) % HEAD) // 2
    sign = np.where(np.arange(P) % 2 == 0, -1.0, 1.0).astype(np.float32)[:, None]
    scale = np.array([HEAD ** -0.5, 1.0], np.float32)[None, :, None]
    cos = np.cos(angle).astype(np.float32).T[pair][:, None, :] * scale
    sin = (np.sin(angle).astype(np.float32).T[pair] * sign)[:, None, :] * scale
    behind = np.arange(P)[None, :] > np.arange(P)[:, None]
    select = np.repeat(np.eye(EXPERTS, dtype=np.float32), P, axis=1)
    return {"c_select": select, "c_cos": cos, "c_sin": sin, "c_mask": np.where(behind, NEG, 0.0).astype(np.float32),
            "c_columns": columns, "c_ident": np.eye(P, dtype=np.float32)}


def lay_out(inputs):
    x = np.asarray(inputs["x"])
    padded = np.zeros((BATCH, TOK // (FREQ // PATCH) * PATCH, FREQ), np.float32)
    padded[:, :TIME] = x
    p = padded.reshape(BATCH, -1, PATCH, FREQ // PATCH, PATCH).transpose(2, 4, 0, 1, 3)
    a = {"patches": np.ascontiguousarray(p.reshape(2, P, TOKENS).transpose(1, 0, 2))}
    v = np.stack([np.asarray(inputs[name]) for name in VECTORS])
    a["vectors"] = np.ascontiguousarray(v.reshape(len(VECTORS), HALVES, P).transpose(2, 0, 1))
    w13 = np.concatenate([np.asarray(inputs[n]).reshape(EXPERTS, 2, P, FFN).transpose(0, 2, 1, 3).reshape(EXPERTS, P, -1)
                          for n in ("L0_ffn_w1", "L0_ffn_w3")], axis=2)
    w2 = np.asarray(inputs["L0_ffn_w2"]).reshape(EXPERTS, FFN // P, P, DIM).transpose(0, 2, 1, 3).reshape(EXPERTS, P, -1)
    a["experts"] = np.concatenate([w13, w2], axis=2)
    a["router_b"] = np.tile(np.asarray(inputs["L0_ffn_router_b"]), (P, 1))
    moved = ("x", "L0_ffn_w1", "L0_ffn_w3", "L0_ffn_w2", "L0_ffn_router_b")
    for name, v in inputs.items():
        if name not in moved and name not in VECTORS:
            a[name] = np.ascontiguousarray(np.asarray(v))
    return a


def kernel(**inputs):
    import concourse.bacc as bacc
    from concourse.bass_utils import run_bass_kernel_spmd

    nc = bacc.Bacc("TRN2", target_bir_lowering=False, num_devices=1)
    arrays = {f"in_{name}": v for name, v in {**lay_out(inputs), **constants()}.items()}
    args = {name: nc.dram_tensor(name, v.shape, mybir.dt.from_np(v.dtype), kind="ExternalInput").ap()
            for name, v in arrays.items()}
    out = nc.dram_tensor("out_features", (P, HALVES, TOKENS), F32, kind="ExternalOutput").ap()
    audio_tower(nc, {name[3:]: v for name, v in args.items()}, out)
    got = run_bass_kernel_spmd(nc, [arrays], core_ids=[0]).results[0]["out_features"]
    return np.ascontiguousarray(got.transpose(2, 1, 0).reshape(BATCH, TOK, DIM))
```
